# Optimizing a Trainium2 kernel written in Bass

```python
import numpy as np
import jax
import jax.numpy as jnp

def _softmax(x, axis=-1):
    return jax.nn.softmax(x, axis=axis)

def _gelu(x):
    return jax.nn.gelu(x, approximate=True)

def _silu(x):
    return jax.nn.silu(x)

def _sigmoid(x):
    return jax.nn.sigmoid(x)

def _layernorm(x, axis=-1, eps=1e-05):
    m = jnp.mean(x, axis=axis, keepdims=True)
    v = jnp.var(x, axis=axis, keepdims=True)
    return (x - m) / jnp.sqrt(v + eps)

def _scatter_add(tgt, idx, src, axis=0):
    return tgt.at[idx].add(src)

def _segment_sum(src, seg, n):
    return jax.ops.segment_sum(src, seg, n)
kernel_name = 'mk_gnn_preln_d2_gnn_r32_82bd08'

def setup_inputs(seed: int=0):
    np.random.seed(seed)
    _w = jnp.asarray

    def _rec_inputs():
        import jax
        import jax.numpy as jnp
        _gk = jax.random.key(seed)
        x = -0.000202 + 1 * jax.random.normal(jax.random.fold_in(_gk, 1), (50000, 128), jnp.float32)
        src = jax.random.randint(jax.random.fold_in(_gk, 2), (50000,), 0, 50000, jnp.int32)
        dst = jax.random.randint(jax.random.fold_in(_gk, 3), (50000,), 0, 50000, jnp.int32)
        _o = jnp.argsort(dst, stable=True)
        src = src[_o]
        dst = dst[_o]
        edge_attr_64 = 0.000149146 + 1.0001 * jax.random.normal(jax.random.fold_in(_gk, 12), (50000, 64), jnp.float32)
        edge_weight = jax.random.uniform(jax.random.fold_in(_gk, 14), (50000,), jnp.float32, 0.0, 999.998)
        node_vec = jax.random.uniform(jax.random.fold_in(_gk, 15), (50000,), jnp.float32, 0.0, 999.994)
        return (x, src, dst, edge_attr_64, edge_weight, node_vec)
    x, src, dst, edge_attr_64, edge_weight, node_vec = _rec_inputs()

    def _L0_gnn_setup():
        import jax, jax.numpy as jnp
        import numpy as np
        N_NODES = 50000
        N_EDGES = 25000
        D = 128
        EPS = 1e-05

        def _layernorm(x, g, b):
            mu = jnp.mean(x, axis=-1, keepdims=True)
            var = jnp.mean(jnp.square(x - mu), axis=-1, keepdims=True)
            return (x - mu) * jax.lax.rsqrt(var + EPS) * g + b
        key = jax.random.key(seed)
        ks = jax.random.split(key, 8)
        feats = jax.random.normal(ks[0], (N_NODES, D), dtype=jnp.float32)
        edge_src = jax.random.randint(ks[1], (N_EDGES,), 0, N_NODES)
        edge_dst = jax.random.randint(ks[2], (N_EDGES,), 0, N_NODES)
        s = 1.0 / np.sqrt(D)
        W0 = jax.random.uniform(ks[3], (D, D), jnp.float32, -s, s)
        W1 = jax.random.uniform(ks[4], (D, D), jnp.float32, -s, s)
        W2 = jax.random.uniform(ks[5], (D, D), jnp.float32, -s, s)
        b0 = jnp.zeros((D,), jnp.float32)
        b1 = jnp.zeros((D,), jnp.float32)
        b2 = jnp.zeros((D,), jnp.float32)
        g0 = jnp.ones((D,), jnp.float32)
        be0 = jnp.zeros((D,), jnp.float32)
        g1 = jnp.ones((D,), jnp.float32)
        be1 = jnp.zeros((D,), jnp.float32)
        return dict(feats=feats, edge_src=edge_src, edge_dst=edge_dst, W0=W0, b0=b0, W1=W1, b1=b1, W2=W2, b2=b2, g0=g0, be0=be0, g1=g1, be1=be1)
    _L0_gnn_all = _L0_gnn_setup()
    _L0_gnn_in = {k: v for k, v in _L0_gnn_all.items() if k in ('W0', 'b0', 'W1', 'b1', 'W2', 'b2', 'g0', 'be0', 'g1', 'be1')}
    del _L0_gnn_all

    def _L1_gnn_setup():
        import jax, jax.numpy as jnp
        import numpy as np
        N = 3125
        E = 20000
        IN_CH = 128
        OUT_CH = 128
        MSG_DIM = 64
        TIME_DIM = 64
        EDGE_DIM = MSG_DIM + TIME_DIM
        HEADS = 4

        def _linear_params(key, fan_in, fan_out, bias=True, scale=0.02):
            k1, k2 = jax.random.split(key)
            W = jax.random.normal(k1, (fan_in, fan_out), jnp.float32) * scale
            if bias:
                b = jax.random.normal(k2, (fan_out,), jnp.float32) * scale
                return (W, b)
            return W

        def transformer_conv(x, src, dst, edge_attr, Wq, bq, Wk, bk, Wv, bv, We, Wskip, bskip):
            n = x.shape[0]
            HC = Wq.shape[1]
            C = HC // HEADS
            q = (x @ Wq + bq).reshape(n, HEADS, C)
            k = (x @ Wk + bk).reshape(n, HEADS, C)
            v = (x @ Wv + bv).reshape(n, HEADS, C)
            e = (edge_attr @ We).reshape(-1, HEADS, C)
            k_j = k[src] + e
            v_j = v[src] + e
            alpha = jnp.einsum('ehc,ehc->eh', q[dst], k_j) / jnp.sqrt(jnp.float32(C))
            amax = jax.ops.segment_max(alpha, dst, num_segments=n)
            expa = jnp.exp(alpha - amax[dst])
            denom = jax.ops.segment_sum(expa, dst, num_segments=n)
            attn = expa / (denom[dst] + 1e-16)
            out = jax.ops.segment_sum(attn[:, :, None] * v_j, dst, num_segments=n)
            out = out.reshape(n, HC)
            return out + x @ Wskip + bskip
        key = jax.random.key(seed)
        ks = jax.random.split(key, 16)
        inp = {'x': jax.random.normal(ks[0], (N, IN_CH), jnp.float32), 'last_update': jax.random.uniform(ks[1], (N,), jnp.float32) * 1000.0, 't': jax.random.uniform(ks[2], (E,), jnp.float32) * 1000.0, 'msg': jax.random.normal(ks[3], (E, MSG_DIM), jnp.float32), 'edge_index': jax.random.randint(ks[4], (2, E), 0, N, jnp.int64)}
        inp['Wt'], inp['bt'] = _linear_params(ks[5], 1, TIME_DIM)
        HC1 = HEADS * (IN_CH // 4)
        inp['Wq1'], inp['bq1'] = _linear_params(ks[6], IN_CH, HC1)
        inp['Wk1'], inp['bk1'] = _linear_params(ks[7], IN_CH, HC1)
        inp['Wv1'], inp['bv1'] = _linear_params(ks[8], IN_CH, HC1)
        inp['We1'] = _linear_params(ks[9], EDGE_DIM, HC1, bias=False)
        inp['Wskip1'], inp['bskip1'] = _linear_params(ks[10], IN_CH, HC1)
        HC2 = HEADS * (OUT_CH // 4)
        inp['Wq2'], inp['bq2'] = _linear_params(ks[11], IN_CH, HC2)
        inp['Wk2'], inp['bk2'] = _linear_params(ks[12], IN_CH, HC2)
        inp['Wv2'], inp['bv2'] = _linear_params(ks[13], IN_CH, HC2)
        inp['We2'] = _linear_params(ks[14], EDGE_DIM, HC2, bias=False)
        inp['Wskip2'], inp['bskip2'] = _linear_params(ks[15], IN_CH, HC2)
        return inp
    _L1_gnn_all = _L1_gnn_setup()
    _L1_gnn_in = {k: v for k, v in _L1_gnn_all.items() if k in ('Wt', 'bt', 'Wq1', 'bq1', 'Wk1', 'bk1', 'Wv1', 'bv1', 'We1', 'Wskip1', 'bskip1', 'Wq2', 'bq2', 'Wk2', 'bk2', 'Wv2', 'bv2', 'We2', 'Wskip2', 'bskip2')}
    del _L1_gnn_all
    return {'x': x, 'src': src, 'dst': dst, 'edge_attr_64': edge_attr_64, 'edge_weight': edge_weight, 'node_vec': node_vec, 'L0_gnn_W0': _L0_gnn_in['W0'], 'L0_gnn_b0': _L0_gnn_in['b0'], 'L0_gnn_W1': _L0_gnn_in['W1'], 'L0_gnn_b1': _L0_gnn_in['b1'], 'L0_gnn_W2': _L0_gnn_in['W2'], 'L0_gnn_b2': _L0_gnn_in['b2'], 'L0_gnn_g0': _L0_gnn_in['g0'], 'L0_gnn_be0': _L0_gnn_in['be0'], 'L0_gnn_g1': _L0_gnn_in['g1'], 'L0_gnn_be1': _L0_gnn_in['be1'], 'L1_gnn_Wt': _L1_gnn_in['Wt'], 'L1_gnn_bt': _L1_gnn_in['bt'], 'L1_gnn_Wq1': _L1_gnn_in['Wq1'], 'L1_gnn_bq1': _L1_gnn_in['bq1'], 'L1_gnn_Wk1': _L1_gnn_in['Wk1'], 'L1_gnn_bk1': _L1_gnn_in['bk1'], 'L1_gnn_Wv1': _L1_gnn_in['Wv1'], 'L1_gnn_bv1': _L1_gnn_in['bv1'], 'L1_gnn_We1': _L1_gnn_in['We1'], 'L1_gnn_Wskip1': _L1_gnn_in['Wskip1'], 'L1_gnn_bskip1': _L1_gnn_in['bskip1'], 'L1_gnn_Wq2': _L1_gnn_in['Wq2'], 'L1_gnn_bq2': _L1_gnn_in['bq2'], 'L1_gnn_Wk2': _L1_gnn_in['Wk2'], 'L1_gnn_bk2': _L1_gnn_in['bk2'], 'L1_gnn_Wv2': _L1_gnn_in['Wv2'], 'L1_gnn_bv2': _L1_gnn_in['bv2'], 'L1_gnn_We2': _L1_gnn_in['We2'], 'L1_gnn_Wskip2': _L1_gnn_in['Wskip2'], 'L1_gnn_bskip2': _L1_gnn_in['bskip2']}

def reference(x, src, dst, edge_attr_64, edge_weight, node_vec, L0_gnn_W0, L0_gnn_b0, L0_gnn_W1, L0_gnn_b1, L0_gnn_W2, L0_gnn_b2, L0_gnn_g0, L0_gnn_be0, L0_gnn_g1, L0_gnn_be1, L1_gnn_Wt, L1_gnn_bt, L1_gnn_Wq1, L1_gnn_bq1, L1_gnn_Wk1, L1_gnn_bk1, L1_gnn_Wv1, L1_gnn_bv1, L1_gnn_We1, L1_gnn_Wskip1, L1_gnn_bskip1, L1_gnn_Wq2, L1_gnn_bq2, L1_gnn_Wk2, L1_gnn_bk2, L1_gnn_Wv2, L1_gnn_bv2, L1_gnn_We2, L1_gnn_Wskip2, L1_gnn_bskip2):
    import jax
    import jax.numpy as jnp

    def _L0_gnn_ref(feats, edge_src, edge_dst, W0, b0, W1, b1, W2, b2, g0, be0, g1, be1):
        import jax, jax.numpy as jnp
        import numpy as np
        N_NODES = 50000
        N_EDGES = 25000
        D = 128
        EPS = 1e-05

        def _layernorm(x, g, b):
            mu = jnp.mean(x, axis=-1, keepdims=True)
            var = jnp.mean(jnp.square(x - mu), axis=-1, keepdims=True)
            return (x - mu) * jax.lax.rsqrt(var + EPS) * g + b
        N = feats.shape[0]
        deg = jax.ops.segment_sum(jnp.ones((edge_dst.shape[0],), feats.dtype), edge_dst, num_segments=N)
        inv = 1.0 / (deg + 1.0)

        def sage_gcn(h, W, b):
            agg = jax.ops.segment_sum(h[edge_src], edge_dst, num_segments=N)
            agg = (agg + h) * inv[:, None]
            return agg @ W + b
        h = sage_gcn(feats, W0, b0)
        h = jax.nn.relu(_layernorm(h, g0, be0))
        h = sage_gcn(h, W1, b1)
        h = jax.nn.relu(_layernorm(h, g1, be1))
        h = sage_gcn(h, W2, b2)
        return h

    def _L1_gnn_ref(x, last_update, t, msg, edge_index, Wt, bt, Wq1, bq1, Wk1, bk1, Wv1, bv1, We1, Wskip1, bskip1, Wq2, bq2, Wk2, bk2, Wv2, bv2, We2, Wskip2, bskip2):
        import jax, jax.numpy as jnp
        import numpy as np
        N = 3125
        E = 20000
        IN_CH = 128
        OUT_CH = 128
        MSG_DIM = 64
        TIME_DIM = 64
        EDGE_DIM = MSG_DIM + TIME_DIM
        HEADS = 4

        def _linear_params(key, fan_in, fan_out, bias=True, scale=0.02):
            k1, k2 = jax.random.split(key)
            W = jax.random.normal(k1, (fan_in, fan_out), jnp.float32) * scale
            if bias:
                b = jax.random.normal(k2, (fan_out,), jnp.float32) * scale
                return (W, b)
            return W

        def transformer_conv(x, src, dst, edge_attr, Wq, bq, Wk, bk, Wv, bv, We, Wskip, bskip):
            n = x.shape[0]
            HC = Wq.shape[1]
            C = HC // HEADS
            q = (x @ Wq + bq).reshape(n, HEADS, C)
            k = (x @ Wk + bk).reshape(n, HEADS, C)
            v = (x @ Wv + bv).reshape(n, HEADS, C)
            e = (edge_attr @ We).reshape(-1, HEADS, C)
            k_j = k[src] + e
            v_j = v[src] + e
            alpha = jnp.einsum('ehc,ehc->eh', q[dst], k_j) / jnp.sqrt(jnp.float32(C))
            amax = jax.ops.segment_max(alpha, dst, num_segments=n)
            expa = jnp.exp(alpha - amax[dst])
            denom = jax.ops.segment_sum(expa, dst, num_segments=n)
            attn = expa / (denom[dst] + 1e-16)
            out = jax.ops.segment_sum(attn[:, :, None] * v_j, dst, num_segments=n)
            out = out.reshape(n, HC)
            return out + x @ Wskip + bskip
        src, dst = (edge_index[0], edge_index[1])
        rel_t = last_update[src] - t
        rel_t_enc = jnp.cos(rel_t[:, None] * Wt[0][None, :] + bt)
        edge_attr = jnp.concatenate([rel_t_enc, msg], axis=-1)
        h = transformer_conv(x, src, dst, edge_attr, Wq1, bq1, Wk1, bk1, Wv1, bv1, We1, Wskip1, bskip1)
        return transformer_conv(h, src, dst, edge_attr, Wq2, bq2, Wk2, bk2, Wv2, bv2, We2, Wskip2, bskip2)
    edge_index = jnp.stack([src, dst])
    h = jnp.maximum(_layernorm(x, axis=-1), 0.0)
    x = x + _L0_gnn_ref(h, src, dst, L0_gnn_W0, L0_gnn_b0, L0_gnn_W1, L0_gnn_b1, L0_gnn_W2, L0_gnn_b2, L0_gnn_g0, L0_gnn_be0, L0_gnn_g1, L0_gnn_be1)
    h = jnp.maximum(_layernorm(x, axis=-1), 0.0)
    x = x + _L1_gnn_ref(h, node_vec, edge_weight, edge_attr_64, edge_index, L1_gnn_Wt, L1_gnn_bt, L1_gnn_Wq1, L1_gnn_bq1, L1_gnn_Wk1, L1_gnn_bk1, L1_gnn_Wv1, L1_gnn_bv1, L1_gnn_We1, L1_gnn_Wskip1, L1_gnn_bskip1, L1_gnn_Wq2, L1_gnn_bq2, L1_gnn_Wk2, L1_gnn_bk2, L1_gnn_Wv2, L1_gnn_bv2, L1_gnn_We2, L1_gnn_Wskip2, L1_gnn_bskip2)
    return x

_drawn_inputs = setup_inputs


def setup_inputs(seed=0):
    import zlib

    import numpy as np

    out = dict(_drawn_inputs(seed))
    spreads = {'L0_gnn_b0': (0.0, 0.1),
     'L0_gnn_b1': (0.0, 0.1),
     'L0_gnn_b2': (0.0, 0.1),
     'L0_gnn_g0': (1.0, 0.2),
     'L0_gnn_be0': (0.0, 0.273),
     'L0_gnn_g1': (1.0, 0.2),
     'L0_gnn_be1': (0.0, 0.1)}
    factors = {'L1_gnn_bt': 37.732,
     'L1_gnn_Wq1': 33.918,
     'L1_gnn_bq1': 172.128,
     'L1_gnn_Wk1': 33.905,
     'L1_gnn_bk1': 200.0,
     'L1_gnn_bv1': 8.0,
     'L1_gnn_bskip1': 8.0,
     'L1_gnn_Wq2': 35.801,
     'L1_gnn_bq2': 64.0,
     'L1_gnn_Wk2': 39.333,
     'L1_gnn_bk2': 200.0,
     'L1_gnn_bv2': 3.791,
     'L1_gnn_bskip2': 3.372}
    for name, (base, spread) in spreads.items():
        noise = np.random.default_rng([zlib.crc32(name.encode()), seed]).standard_normal(out[name].shape)
        drawn = base * np.exp(spread * noise) if base else spread * noise
        out[name] = jnp.asarray(drawn.astype(out[name].dtype))
    for name, factor in factors.items():
        out[name] = (out[name] * factor).astype(out[name].dtype)
    return out
```

```python
import math
from contextlib import ExitStack

import concourse.bass as bass
from concourse import mybir

F32 = mybir.dt.float32
I32 = mybir.dt.int32
U32 = mybir.dt.uint32
ALU = mybir.AluOpType
ACT = mybir.ActivationFunctionType
AX = mybir.AxisListType

P = 128
NJ = 8
EG = 7
HALF = NJ // 2
BANK = 512
HEADS = 4
EPS = 1e-5
W0COLS = 132
BIG = 1.0e38
NO_NODE = 65536
MAGIC = 1.5 * 2.0 ** 23
TWO_PI_HI = 6.28125
TWO_PI_LO = 2.0 * math.pi - TWO_PI_HI


class Steps:

    def __init__(self, sem, per_group):
        self.sem, self.per_group = sem, per_group

    def start(self, g):
        self.g, self.k = g, 0

    def mark(self, ins):
        ins.then_inc(self.sem, 1)
        self.k += 1

    def wait(self, eng):
        eng.wait_ge(self.sem, self.g * self.per_group + self.k)

    def end(self):
        assert self.k == self.per_group, (self.k, self.per_group)


class State:
    pass


def fresh_semaphores(nc, st, names, primed=None, gpsimd_dma=()):
    assert len(names) <= len(st.pool)
    nc.gpsimd.sem_clear(range(st.pool[0].num, st.pool[-1].num + 1))
    sems = dict(zip(names, st.pool))
    for name, credit in (primed or {}).items():
        nc.gpsimd.sem_inc(sems[name], credit)
    nc.all_engine_barrier()
    for name in gpsimd_dma:
        sems[name] = st.ctx.enter_context(nc.semaphore(f"{name}_{st.phase}"))
    return sems


def setup_phase(nc, st, a):
    N, E, EC, NR = st.N, st.E, st.EC, st.NR
    full = E // EC
    rest = E - full * EC
    s = fresh_semaphores(nc, st, ["fill", "load", "load2", "zero", "step", "diag", "bc", "diag2", "tri", "msgpad"])
    with ExitStack() as ctx:
        sb = lambda n, sh, d=F32: ctx.enter_context(nc.sbuf_tensor(n, sh, d))
        dst_i = sb("dst_i", [P, EC], I32)
        zeros = sb("zeros", [P, EC * W0COLS // 8])
        next_i = sb("next_i", [P, 1], I32)
        nextf = sb("nextf", [P, 1])
        lastf = sb("lastf", [P, EC])
        tmp = sb("tmp", [P, EC])
        diag = sb("diag", [P, 2, P])
        ends = sb("ends", [P, 4])
        block = ctx.enter_context(nc.Block())
        n_w = 0

        @block.gpsimd
        def _(pool):
            nc.gpsimd.memset(zeros[:, :], 0.0).then_inc(s["fill"], 1)
            nc.gpsimd.memset(st.src_i[:, :], 0).then_inc(s["fill"], 1)
            nc.gpsimd.memset(dst_i[:, :], NO_NODE).then_inc(s["fill"], 1)
            nc.gpsimd.memset(next_i[:, :], NO_NODE + 1).then_inc(s["fill"], 1)
            nc.gpsimd.memset(st.ew[:, :], 0.0).then_inc(s["fill"], 1)
            nc.gpsimd.memset(st.nv[:, :], 0.0).then_inc(s["fill"], 1)
            nc.gpsimd.memset(st.ident[:, :], 0.0).then_inc(s["fill"], 1)
            nc.gpsimd.memset(st.tri[:, :], 1.0).then_inc(s["fill"], 1)
            nc.gpsimd.memset(st.ones[:, :], 1.0).then_inc(s["fill"], 1)
            nc.gpsimd.memset(st.eps[:, :], EPS).then_inc(s["fill"], 1)
            nc.gpsimd.memset(st.half_pi[:, :], math.pi / 2).then_inc(s["fill"], 1)
            pool.wait_ge(s["fill"], 11)
            nc.gpsimd.affine_select(out=st.ident[:, :], in_=st.ident[:, :], compare_op=ALU.not_equal, fill=1.0,
                                    base=0, pattern=[[-1, P]], channel_multiplier=1).then_inc(s["tri"], 1)
            nc.gpsimd.affine_select(out=st.tri[:, :], in_=st.tri[:, :], compare_op=ALU.is_gt, fill=0.0,
                                    base=0, pattern=[[1, P]], channel_multiplier=-1).then_inc(s["tri"], 1)

        @block.sync
        def _(sp):
            nonlocal n_w
            plain = [(st.w[0], a["L0_gnn_W0"]), (st.w[1], a["L0_gnn_W1"]), (st.w[2], a["L0_gnn_W2"])]
            for c in range(2):
                for j, name in enumerate(("Wk", "Wv", "Wq", "Wskip")):
                    plain.append((st.w4[:, c, j * P:(j + 1) * P], a[f"L1_gnn_{name}{c + 1}"]))
                    bias = a[f"L1_gnn_b{name[1:]}{c + 1}"]
                    plain.append((st.b4[:, c, j * P:(j + 1) * P],
                                  bias.rearrange("(o n) -> o n", o=1).broadcast_to([P, P])))
                plain.append((st.we[:, c * P:(c + 1) * P], a[f"L1_gnn_We{c + 1}"]))
            for layer in range(3):
                plain.append((st.b0[:, layer, :],
                              a[f"L0_gnn_b{layer}"].rearrange("(o n) -> o n", o=1).broadcast_to([P, P])))
            for j, name in enumerate(("g0", "be0", "g1", "be1")):
                plain.append((st.gb[:, j:j + 1], a[f"L0_gnn_{name}"].rearrange("(n o) -> n o", o=1)))
            TD = st.TD
            plain.append((st.wt[:, :], a["L1_gnn_Wt"].broadcast_to([P, TD])))
            plain.append((st.bt[:, :], a["L1_gnn_bt"].rearrange("(o n) -> o n", o=1).broadcast_to([P, TD])))
            for dst, src in plain:
                sp.dma_start(dst if isinstance(dst, bass.AP) else dst[:, :], src).then_inc(s["load"], 16)
            n_w = len(plain)
            sp.wait_ge(s["fill"], 11)
            edge_lists = [(st.src_i, a["src"]), (dst_i, a["dst"]), (st.ew, a["edge_weight"])]
            for tile, flat in edge_lists:
                sp.dma_start(tile[0:full, :],
                             flat[0:full * EC].rearrange("(p t) -> p t", t=EC)).then_inc(s["load2"], 16)
                sp.dma_start(tile[full:full + 1, 0:rest],
                             flat[full * EC:E].rearrange("(o t) -> o t", o=1)).then_inc(s["load2"], 16)
            with nc.allow_non_contiguous_dma(reason="one element per partition"):
                sp.dma_start(next_i[0:full, :],
                             a["dst"][EC:EC + (full - 1) * EC + 1:EC].rearrange("(p o) -> p o", o=1)
                             ).then_inc(s["load2"], 16)
            G, tail = st.NGROUPS - 1, st.TAILP
            nvv = st.nv[:, :].rearrange("p (g j) -> p g j", j=NJ)
            sp.dma_start(nvv[:, 0:G, :],
                         a["node_vec"][0:G * P * NJ].rearrange("(g p j) -> p g j", p=P, j=NJ)
                         ).then_inc(s["load2"], 16)
            sp.dma_start(nvv[0:tail, G, :],
                         a["node_vec"][G * P * NJ:N].rearrange("(p j) -> p j", j=NJ)).then_inc(s["load2"], 16)
            sp.wait_ge(s["load"], 16 * n_w)
            sp.wait_ge(s["load2"], 16 * 9)

        @block.scalar
        def _(act):
            act.dma_start(st.msg[0:E, :].rearrange("(p r) d -> p (r d)", p=16),
                          a["edge_attr_64"].rearrange("(p r) d -> p (r d)", p=16),
                          max_dma_last_dim=32768).then_inc(s["msgpad"], 16)
            act.wait_ge(s["fill"], 11)
            pad = (P * EC - E) * st.MD // 16
            act.dma_start(st.msg[E:P * EC, :].rearrange("(p r) d -> p (r d)", p=16),
                          zeros[0:16, 0:pad]).then_inc(s["msgpad"], 16)
            n = 0
            for table, width in ((st.agg0, W0COLS), (st.agg, P)):
                view = table.rearrange("(p r) d -> p (r d)", p=P)
                piece = EC * width // 8
                for k in range(8):
                    act.dma_start(view[:, k * piece:(k + 1) * piece], zeros[:, 0:piece]).then_inc(s["zero"], 16)
                    n += 1
            act.wait_ge(s["zero"], 16 * n)
            act.wait_ge(s["msgpad"], 32)

        @block.vector
        def _(dve):
            chain = Steps(s["step"], 99)
            chain.start(0)

            def link(ins):
                chain.mark(ins)
                chain.wait(dve)

            dve.wait_ge(s["load2"], 16 * 9)
            link(nc.vector.tensor_copy(st.dstf[:, :], dst_i[:, :]))
            link(nc.vector.tensor_copy(nextf[:, :], next_i[:, :]))
            link(nc.vector.memset(st.cont[:, 0:1], 0.0))
            link(nc.vector.tensor_tensor(st.cont[:, 1:EC], st.dstf[:, 1:EC], st.dstf[:, 0:EC - 1], ALU.is_equal))
            link(nc.vector.memset(st.contn[:, EC - 1:EC], 0.0))
            link(nc.vector.tensor_scalar(st.contn[:, 0:EC - 1], st.cont[:, 1:EC], 1.0, None, ALU.mult))
            link(nc.vector.tensor_tensor(lastf[:, 0:EC - 1], st.dstf[:, 0:EC - 1], st.dstf[:, 1:EC], ALU.not_equal))
            link(nc.vector.tensor_tensor(lastf[:, EC - 1:EC], st.dstf[:, EC - 1:EC], nextf[:, :], ALU.not_equal))
            link(nc.vector.tensor_scalar(tmp[:, :], lastf[:, :], -float(NO_NODE), float(NO_NODE),
                                         ALU.mult, ALU.add))
            link(nc.vector.tensor_tensor(tmp[:, :], tmp[:, :], st.dstf[:, :], ALU.add))
            link(nc.vector.tensor_copy(st.sidx_i[:, :], tmp[:, :]))
            link(nc.vector.tensor_scalar(tmp[:, :], st.dstf[:, :], float(N - 1), None, ALU.min))
            link(nc.vector.tensor_copy(st.qidx_i[:, :], tmp[:, :]))
            link(nc.vector.tensor_scalar(st.pen[:, :], st.cont[:, :], BIG, -BIG, ALU.mult, ALU.add))
            link(nc.vector.tensor_scalar(st.penn[:, :], st.contn[:, :], BIG, -BIG, ALU.mult, ALU.add))
            first, last = st.dstf[:, 0:1], st.dstf[:, EC - 1:EC]
            link(nc.vector.tensor_scalar(st.in_first[:, :], st.dstf[:, :], first, None, ALU.is_equal))
            link(nc.vector.tensor_scalar(st.in_last[:, :], st.dstf[:, :], last, None, ALU.is_equal))
            link(nc.vector.tensor_tensor(ends[:, 0:1], first, last, ALU.not_equal))
            link(nc.vector.tensor_scalar(st.two_ended[:, :], ends[:, 0:1], 1.0, None, ALU.mult))
            link(nc.vector.tensor_tensor(ends[:, 1:2], ends[:, 0:1], lastf[:, EC - 1:EC], ALU.max))
            link(nc.vector.tensor_scalar(ends[:, 2:3], ends[:, 1:2], -float(NO_NODE), float(NO_NODE),
                                         ALU.mult, ALU.add))
            link(nc.vector.tensor_tensor(ends[:, 3:4], ends[:, 2:3], first, ALU.add))
            link(nc.vector.tensor_copy(st.carry_to[:, :], ends[:, 3:4]))
            link(nc.vector.tensor_copy(st.carry_from[:, :], first))
            dve.wait_ge(s["tri"], 2)
            link(nc.vector.tensor_scalar(diag[:, 0, :], st.ident[:, :], first, None, ALU.mult))
            chain.mark(nc.vector.tensor_scalar(diag[:, 1, :], st.ident[:, :], last, None, ALU.mult))
            dve.sem_inc(s["diag2"], 1)
            chain.wait(dve)
            nc.vector.memset(ends[:, 0:1], 0.0).then_inc(s["diag"], 1)
            dve.wait_ge(s["bc"], 1)
            for m, (row, col) in enumerate(((0, first), (1, first), (0, last), (1, last))):
                link(nc.vector.tensor_scalar(st.same[:, m, :], st.psA[:, 0, row * P:(row + 1) * P], col, None,
                                             ALU.is_equal))
            link(nc.vector.tensor_tensor(st.carry[:, :], st.same[:, 2, :], st.tri[:, :], ALU.mult))
            link(nc.vector.tensor_scalar(st.pen_same[:, :, :], st.same[:, :, :], BIG, -BIG, ALU.mult, ALU.add))

        @block.tensor
        def _(pe):
            pe.wait_ge(s["diag"], 1)
            nc.tensor.matmul(st.psA[:, 0, 0:P], st.ones[:, :], diag[:, 0, :], start=True, stop=True)
            nc.tensor.matmul(st.psA[:, 0, P:2 * P], st.ones[:, :], diag[:, 1, :],
                             start=True, stop=True).then_inc(s["bc"], 1)


def pipelined(eng, groups, stages, hi=None):
    deepest = max(lag for _, lag in stages)
    lo = -(-deepest // 2)
    hi = groups // 2 if hi is None else hi

    def step(k):
        for body, lag in stages:
            if 0 <= k - lag < groups:
                body(k - lag, (k - lag) % 2, (k - lag) // 2)

    for k in range(2 * lo):
        step(k)
    with eng.Fori(lo, hi) as pair:
        for c in range(2):
            for body, lag in stages:
                d = (c - lag) // 2
                body(2 * pair + (c - lag), (c - lag) % 2, pair + d if d else pair)
    for k in range(2 * hi, groups + deepest):
        step(k)


def node_phase(nc, st, kind, agg=None, add=None, resid=None, bias=None, w=None, wide=None, affine=None,
               stores=(), final=None, first_table=False):
    N, NR, G = st.N, st.NR, st.NGROUPS - 1
    norm = kind in ("first", "deg", "sage")
    sage = kind in ("deg", "sage")
    nload = (agg is not None) + (add is not None) + (resid is not None)
    wide_n = wide is not None
    units = NJ if wide_n else NJ // HALF
    ocols = BANK if wide_n else (W0COLS if first_table else P)
    names = ["loaded0", "loaded1", "z_ready", "step", "stats", "std", "normed", "tposed", "h_ready", "y_done",
             "y_out", "nv_put", "stored0", "stored1", "z_out", "z_stored0", "z_stored1", "ones",
             "fence", "o_free", "z_free", "taken", "step_b"]
    nst = len(stores)
    primed = dict(z_ready=2, normed=2 * NJ, tposed=2 * NJ, h_ready=4, y_done=2 * units, y_out=4,
                  o_free=2, z_free=2, taken=2)
    s = fresh_semaphores(nc, st, names, primed)
    loaded = (s["loaded0"], s["loaded1"])
    stored = (s["stored0"], s["stored1"])
    z_stored = (s["z_stored0"], s["z_stored1"])
    acols = W0COLS if kind == "deg" else P
    ycols = W0COLS if kind == "deg" else P
    grouped = lambda t: t.rearrange("(g p j) d -> p g j d", p=P, j=NJ)

    with ExitStack() as ctx:
        sb = lambda n, sh, d=F32: ctx.enter_context(nc.sbuf_tensor(f"{n}_{st.phase}", sh, d))
        A = sb("A", [P, 2, NJ, acols]) if agg is not None else None
        Y = sb("Y", [P, 2, NJ, ycols]) if add is not None else None
        X = sb("X", [P, 2, NJ, P]) if resid is not None else None
        Z = sb("Z", [P, 2, NJ, P])
        S = sb("S", [P, 2, NJ, P]) if sage else Z
        nrm = sb("nrm", [P, 2, NJ, P]) if norm else Z
        bn = sb("bn", [P, 2, NJ, 6])
        mv = sb("mv", [P, 2, NJ, 2])
        std = sb("std", [P, 2, NJ])
        rstd = sb("rstd", [P, 2, NJ])
        deg1 = sb("deg1", [P, 2, NJ])
        inv = sb("inv", [P, 2, NJ])
        hT = sb("hT", [P, 2, NJ * P]) if kind != "final" else None
        O = sb("O", [P, 2, NJ, ocols]) if kind != "final" else None
        psA, psB = st.psA, st.psB
        block = ctx.enter_context(nc.Block())

        def load(sp, g, slot, tail):
            for tile, table in ((A, agg), (Y, add), (X, resid)):
                if tile is None:
                    continue
                if table.shape[0] == N and tail:
                    src = table[G * P * NJ:N, :].rearrange("(p j) d -> p j d", j=NJ)
                    sp.dma_start(tile[0:st.TAILP, slot, :, :], src).then_inc(loaded[slot], 16)
                else:
                    src = grouped(table[0:G * P * NJ, :]) if table.shape[0] == N else grouped(table)
                    sp.dma_start(tile[:, slot:slot + 1, :, :].rearrange("p g j d -> p g (j d)"),
                                 src[:, bass.ds(g, 1), :, :].rearrange("p g j d -> p g (j d)")
                                 ).then_inc(loaded[slot], 16)

        def consumed(sp, g):
            if final is not None:
                sp.wait_ge(s["z_out"], g + 1)
            elif sage:
                sp.wait_ge(s["taken"], g + 3)
            else:
                sp.wait_ge(s["z_ready"], g + 3)

        @block.sync
        def _(sp):
            def z_out(g, slot, i):
                sp.wait_ge(s["z_out"], g + 1)
                if final.shape[0] == N and isinstance(g, int) and g == G:
                    sp.dma_start(final[G * P * NJ:N, :].rearrange("(p j) d -> p j d", j=NJ),
                                 Z[0:st.TAILP, slot, :, :]).then_inc(z_stored[slot], 16)
                else:
                    dst = grouped(final[0:G * P * NJ, :]) if final.shape[0] == N else grouped(final)
                    sp.dma_start(dst[:, bass.ds(g, 1), :, :].rearrange("p g j d -> p g (j d)"),
                                 Z[:, slot:slot + 1, :, :].rearrange("p g j d -> p g (j d)")
                                 ).then_inc(z_stored[slot], 16)

            def z_retire(g, slot, i):
                sp.wait_ge(z_stored[slot], 16 * (i + 1))
                sp.sem_inc(s["z_free"], 1)

            def load_next(g, slot, i):
                if isinstance(g, int) and g + 2 > G:
                    return
                consumed(sp, g)
                load(sp, g + 2, slot, isinstance(g, int) and g + 2 == G)

            def y_out(g, slot, i):
                sp.wait_ge(s["y_out"], (g + 1) * units + 4)
                if first_table:
                    sp.wait_ge(s["nv_put"], g + 1)
                for table, lo, hi in stores:
                    sp.dma_start(grouped(table)[:, bass.ds(g, 1), :, :].rearrange("p g j d -> p (g j) d"),
                                 O[:, slot, :, lo:hi]).then_inc(stored[slot], 16)

            def y_retire(g, slot, i):
                sp.wait_ge(stored[slot], 16 * nst * (i + 1))
                sp.sem_inc(s["o_free"], 1)

            load(sp, 0, 0, False)
            load(sp, 1, 1, False)
            stages = [(z_out, 0), (z_retire, 1)] if final is not None else []
            stages.append((load_next, 0))
            if nst:
                stages += [(y_out, 2), (y_retire, 3)]
            pipelined(sp, G + 1, stages, hi=(G - 2) // 2)

        @block.gpsimd
        def _(pool):
            def body(g, slot, i):
                pool.wait_ge(loaded[slot], 16 * nload * (i + 1))
                if sage:
                    pool.wait_ge(s["taken"], g + 1)
                elif kind == "conv":
                    pool.wait_ge(s["tposed"], g * NJ + NJ)
                elif kind == "first":
                    pool.wait_ge(s["normed"], g * NJ + NJ)
                else:
                    pool.wait_ge(s["z_free"], g + 1)
                if kind == "first":
                    pool.sem_inc(s["fence"], 1)
                    ins = nc.gpsimd.tensor_copy(Z[:, slot, :, :], X[:, slot, :, :])
                else:
                    ins = nc.gpsimd.tensor_tensor(S[:, slot, :, :], A[:, slot, :, 0:P], Y[:, slot, :, 0:P], ALU.add)
                ins.then_inc(s["z_ready"], 1)
            pipelined(pool, G + 1, [(body, 0)])

        @block.vector
        def _(dve):
            if first_table:
                for slot in range(2):
                    nc.vector.memset(O[:, slot, :, P + 1:W0COLS], 1.0).then_inc(s["ones"], 1)
                dve.wait_ge(s["ones"], 2)
            chain = Steps(s["step"], (3 if kind == "deg" else 0) + (1 if sage else 0)
                          + (2 * NJ - 1 if norm else 0))
            chain_b = Steps(s["step_b"], 1)
            bcast = lambda ap: ap.unsqueeze(2).broadcast_to([P, NJ, P])

            def statistics(g, slot, i):
                chain.start(g)
                z = Z[:, slot, :, :]
                dve.wait_ge(s["z_ready"], g + 3)
                if kind in ("deg", "final"):
                    dve.wait_ge(loaded[slot], 16 * nload * (i + 1))
                if kind == "deg":
                    chain.mark(nc.vector.tensor_scalar(deg1[:, slot, :], A[:, slot, :, P + 1], 1.0, None, ALU.add))
                    chain.wait(dve)
                    chain.mark(nc.vector.reciprocal(inv[:, slot, :], deg1[:, slot, :]))
                    chain.wait(dve)
                    chain.mark(nc.vector.tensor_scalar(st.inv[:, bass.ds(g * NJ, NJ)], inv[:, slot, :], 1.0, None,
                                                       ALU.mult))
                    chain.wait(dve)
                if sage:
                    dve.wait_ge(s["normed"], g * NJ + NJ)
                    if final is not None:
                        dve.wait_ge(s["z_free"], g + 1)
                    nc.vector.tensor_tensor(z, S[:, slot, :, :], bcast(st.inv[:, bass.ds(g * NJ, NJ)]),
                                            ALU.mult).then_inc(s["taken"], 1)
                    dve.wait_ge(s["taken"], g + 3)
                    chain.mark(nc.vector.tensor_tensor(
                        z, z, st.b0[:, bias, :].unsqueeze(1).broadcast_to([P, NJ, P]), ALU.add))
                    chain.wait(dve)
                if resid is not None and kind != "first":
                    dve.wait_ge(loaded[slot], 16 * nload * (i + 1))
                    nc.vector.tensor_tensor(z, z, X[:, slot, :, :], ALU.add).then_inc(s["z_out"], 1)
                    dve.wait_ge(s["z_out"], g + 1)
                if norm:
                    for j in range(NJ):
                        chain.mark(nc.vector.bn_stats(bn[:, slot, j, :], Z[:, slot, j, :]))
                    chain.wait(dve)
                    dve.sem_inc(s["fence"], 1)
                    for j in range(NJ):
                        ins = nc.vector.bn_aggr(mv[:, slot, j, :], bn[:, slot, j, :])
                        if j < NJ - 1:
                            chain.mark(ins)
                    ins.then_inc(s["stats"], 1)
                    chain.wait(dve)
                chain.end()

            def normalise(g, slot, i):
                chain_b.start(g)
                dve.wait_ge(s["std"], g + 1)
                chain_b.mark(nc.vector.reciprocal(rstd[:, slot, :], std[:, slot, :]))
                chain_b.wait(dve)
                dve.wait_ge(s["tposed"], g * NJ + NJ)
                for j in range(NJ):
                    nc.vector.tensor_scalar(nrm[:, slot, j, :], Z[:, slot, j, :], mv[:, slot, j, 0:1],
                                            rstd[:, slot, j:j + 1], ALU.subtract,
                                            ALU.mult).then_inc(s["normed"], 1)

            def products_out(g, slot, i):
                dve.wait_ge(s["o_free"], g + 1)
                for u in range(units):
                    dve.wait_ge(s["y_done"], g * units + u + 1 + 2 * units)
                    nc.vector.tensor_tensor(O[:, slot, u, :], psB[:, u % 4, :], st.b4[:, wide, :],
                                            ALU.add).then_inc(s["y_out"], 1)

            def node_vec_out(g, slot, i):
                dve.wait_ge(s["o_free"], g + 1)
                nc.vector.tensor_scalar(O[:, slot, :, P], st.nv[:, bass.ds(g * NJ, NJ)], 1.0, None,
                                        ALU.mult).then_inc(s["nv_put"], 1)

            stages = [(statistics, 0)] if norm or kind == "final" else []
            if norm:
                stages.append((normalise, 1))
            if first_table:
                stages.append((node_vec_out, 2))
            if wide_n:
                stages.append((products_out, 2 if norm else 0))
            pipelined(dve, G + 1, stages)

        if kind == "final":
            return

        @block.scalar
        def _(act):
            def deviation(g, slot, i):
                act.wait_ge(s["stats"], g + 1)
                act.activation(std[:, slot, :], mv[:, slot, :, 1], ACT.Sqrt,
                               bias=st.eps[:, 0:1]).then_inc(s["std"], 1)

            def features(g, slot, i):
                for half in range(2):
                    act.wait_ge(s["tposed"], g * NJ + (half + 1) * HALF + 2 * NJ)
                    act.wait_ge(s["y_done"], g * units + units)
                    out = hT[:, slot, half * BANK:(half + 1) * BANK]
                    src = psA[:, 2 * slot + half, :]
                    if kind == "conv":
                        ins = act.activation(out, src, ACT.Copy)
                    elif affine is None:
                        ins = act.activation(out, src, ACT.Relu)
                    else:
                        ins = act.activation(out, src, ACT.Relu, scale=st.gb[:, affine:affine + 1],
                                             bias=st.gb[:, affine + 1:affine + 2])
                    ins.then_inc(s["h_ready"], 1)

            def products_out(g, slot, i):
                act.wait_ge(s["o_free"], g + 1)
                for u in range(units):
                    act.wait_ge(s["y_done"], g * units + u + 1 + 2 * units)
                    act.activation(O[:, slot, HALF * u:HALF * (u + 1), 0:P],
                                   psB[:, 2 * slot + u, :].rearrange("p (j d) -> p j d", d=P),
                                   ACT.Copy).then_inc(s["y_out"], 1)

            stages = [(deviation, 0), (features, 1)] if norm else [(features, 0)]
            if not wide_n:
                stages.append((products_out, 2))
            pipelined(act, G + 1, stages)

        @block.tensor
        def _(pe):
            def transposes(g, slot, i):
                if norm:
                    pe.wait_ge(s["normed"], g * NJ + NJ + 2 * NJ)
                else:
                    pe.wait_ge(s["z_ready"], g + 3)
                pe.wait_ge(s["h_ready"], g * 2 + 2)
                for j in range(NJ):
                    nc.tensor.transpose(psA[:, 2 * slot + j // HALF, (j % HALF) * P:(j % HALF + 1) * P],
                                        nrm[:, slot, j, :], st.ident[:, :]).then_inc(s["tposed"], 1)

            def products(g, slot, i):
                for u in range(units):
                    if u % (units // 2) == 0:
                        pe.wait_ge(s["h_ready"], g * 2 + u // (units // 2) + 1 + 4)
                    pe.wait_ge(s["y_out"], g * units + u + 1)
                    if wide_n:
                        ins = nc.tensor.matmul(psB[:, u % 4, :], hT[:, slot, u * P:(u + 1) * P],
                                               st.w4[:, wide, :], start=True, stop=True)
                    else:
                        for j in range(HALF):
                            t = u * HALF + j
                            ins = nc.tensor.matmul(psB[:, 2 * slot + u, j * P:(j + 1) * P],
                                                   hT[:, slot, t * P:(t + 1) * P], st.w[w][:, :],
                                                   start=True, stop=True)
                    ins.then_inc(s["y_done"], 1)

            pipelined(pe, G + 1, [(transposes, 0), (products, 1)])


def edge_groups(eng, total, body):
    with eng.Fori(0, total // 2) as i:
        for slot in range(2):
            body(2 * i + slot, slot, i)


def segment_sum_phase(nc, st, table, cols, agg, embed=False, take_rel=False, weighted=None):
    EC, NG = st.EC, st.EC // EG
    TD, MD = st.TD, st.MD
    names = ["idx_copied", "sidx_copied", "fence", "summed", "rel", "start",
             "msg0", "msg1", "step", "ang", "tenc", "tposed", "eat", "e_done", "e_out", "e_st0", "e_st1",
             "v0", "v1", "weighted", "tail",
             "sums_free", "eb_free"]
    primed = dict(summed=2 * EG, sums_free=2, rel=2, weighted=2, tenc=2, ang=2, tposed=2 * EG,
                  eat=4, e_done=8, e_out=4, eb_free=2)
    s = fresh_semaphores(nc, st, names, primed, gpsimd_dma=("rows0", "rows1", "scat0", "scat1"))
    rows_in, scat = (s["rows0"], s["rows1"]), (s["scat0"], s["scat1"])
    msg_in, e_st, v_in = (s["msg0"], s["msg1"]), (s["e_st0"], s["e_st1"]), (s["v0"], s["v1"])
    with ExitStack() as ctx:
        sb = lambda n, sh, d=F32: ctx.enter_context(nc.sbuf_tensor(f"{n}_{st.phase}", sh, d))
        gidx = sb("gidx", [P, 2, EG], I32)
        sidx = sb("sidx", [P, 2, EG], I32)
        rows = sb("rows", [P, 2, EG, cols])
        sums = sb("sums", [P, 2, EG, cols])
        V = sb("V", [P, 2, EG, P]) if weighted else None
        if embed:
            EA = sb("EA", [P, 2, EG, TD + MD])
            ang = sb("ang", [P, 2, EG, TD])
            turn = sb("turn", [P, EG, TD])
            eaT = sb("eaT", [P, 2, EG * P])
            EB = sb("EB", [P, 2, EG, 2 * P])
        psA, psB = st.psA, st.psB
        block = ctx.enter_context(nc.Block())

        @block.gpsimd
        def _(pool):
            def gathers(g, slot):
                pool.wait_ge(s["summed"], EG * g + EG)
                if take_rel:
                    pool.wait_ge(s["rel"], g + 1)
                pool.sem_inc(s["fence"], 1)
                nc.gpsimd.tensor_copy(gidx[:, slot, :], st.src_i[:, bass.ds(g * EG, EG)]
                                      ).then_inc(s["idx_copied"], 1)
                pool.wait_ge(s["idx_copied"], g + 1)
                pool.sem_inc(s["fence"], 1)
                for j in range(EG):
                    nc.gpsimd.indirect_dma_start(rows[:, slot, j, :], None, table[:, :],
                                                 bass.IndirectOffsetOnAxis(gidx[:, slot, j:j + 1], 0)
                                                 ).then_inc(rows_in[slot], 16)

            def retire(slot, i):
                pool.wait_ge(scat[slot], 16 * EG * (i + 1))
                pool.sem_inc(s["sums_free"], 1)

            def scatters(g, slot, midway=None):
                nc.gpsimd.tensor_copy(sidx[:, slot, :], st.sidx_i[:, bass.ds(g * EG, EG)]
                                      ).then_inc(s["sidx_copied"], 1)
                pool.wait_ge(s["sidx_copied"], g + 1)
                pool.wait_ge(s["summed"], EG * g + EG + 2 * EG)
                pool.sem_inc(s["fence"], 1)
                for j in range(EG):
                    if j == 3 and midway is not None:
                        retire(*midway)
                    nc.gpsimd.indirect_dma_start(agg[:, :], bass.IndirectOffsetOnAxis(sidx[:, slot, j:j + 1], 0),
                                                 sums[:, slot, j, :], None, bounds_check=st.NR - 1,
                                                 oob_is_err=False).then_inc(scat[slot], 16)

            if weighted:
                scatters(0, 0)
                with pool.Fori(0, NG // 2 - 1) as i:
                    scatters(2 * i + 1, 1, midway=(0, i))
                    scatters(2 * i + 2, 0, midway=(1, i))
                scatters(NG - 1, 1, midway=(0, NG // 2 - 1))
            else:
                gathers(0, 0)
                gathers(1, 1)
                scatters(0, 0)
                with pool.Fori(0, NG // 2 - 1) as i:
                    gathers(2 * i + 2, 0)
                    retire(0, i)
                    scatters(2 * i + 1, 1)
                    gathers(2 * i + 3, 1)
                    retire(1, i)
                    scatters(2 * i + 2, 0)
                retire(0, NG // 2 - 1)
                scatters(NG - 1, 1)
            retire(1, NG // 2 - 1)

        @block.vector
        def _(dve):
            nc.vector.memset(sums[:, 1, EG - 1, :], 0.0).then_inc(s["start"], 1)
            dve.wait_ge(s["start"], 1)
            chain = Steps(s["step"], 6)

            def body(g, slot, i):
                if weighted:
                    dve.wait_ge(v_in[slot], 16 * (i + 1))
                    att = st.alpha[:, :, bass.ds(g * EG, EG)].rearrange("p h t -> p t h")
                    nc.vector.tensor_tensor(rows[:, slot, :, :].rearrange("p t (h c) -> p t h c", h=HEADS),
                                            V[:, slot, :, :].rearrange("p t (h c) -> p t h c", h=HEADS),
                                            att.unsqueeze(3).broadcast_to([P, EG, HEADS, P // HEADS]),
                                            ALU.mult).then_inc(s["weighted"], 1)
                    dve.wait_ge(s["weighted"], g + 3)
                else:
                    dve.wait_ge(rows_in[slot], 16 * EG * (i + 1))
                dve.wait_ge(s["sums_free"], g + 1)
                for j in range(EG):
                    before = sums[:, slot, j - 1, :] if j else sums[:, 1 - slot, EG - 1, :]
                    dve.wait_ge(s["summed"], EG * g + j + 2 * EG)
                    nc.vector.scalar_tensor_tensor(
                        sums[:, slot, j, :], before, st.cont[:, bass.ds(g * EG + j, 1)], rows[:, slot, j, :],
                        ALU.mult, ALU.add).then_inc(s["summed"], 1)
                if take_rel:
                    nc.vector.tensor_tensor(st.rel[:, bass.ds(g * EG, EG)], rows[:, slot, :, P],
                                            st.ew[:, bass.ds(g * EG, EG)], ALU.subtract).then_inc(s["rel"], 1)
                if embed:
                    chain.start(g)
                    a = ang[:, slot, :, :]
                    dve.wait_ge(s["tenc"], g + 1)
                    chain.mark(nc.vector.tensor_tensor(
                        a, st.rel[:, bass.ds(g * EG, EG)].unsqueeze(2).broadcast_to([P, EG, TD]),
                        st.wt[:, :].unsqueeze(1).broadcast_to([P, EG, TD]), ALU.mult))
                    chain.wait(dve)
                    chain.mark(nc.vector.tensor_tensor(
                        a, a, st.bt[:, :].unsqueeze(1).broadcast_to([P, EG, TD]), ALU.add))
                    chain.wait(dve)
                    chain.mark(nc.vector.tensor_scalar(turn[:, :, :], a, 1.0 / (2 * math.pi), MAGIC,
                                                       ALU.mult, ALU.add))
                    chain.wait(dve)
                    chain.mark(nc.vector.tensor_scalar(turn[:, :, :], turn[:, :, :], MAGIC, None, ALU.subtract))
                    chain.wait(dve)
                    chain.mark(nc.vector.scalar_tensor_tensor(a, turn[:, :, :], -TWO_PI_HI, a, ALU.mult, ALU.add))
                    chain.wait(dve)
                    chain.mark(nc.vector.scalar_tensor_tensor(a, turn[:, :, :], -TWO_PI_LO, a, ALU.mult, ALU.add))
                    chain.wait(dve)
                    nc.vector.scalar_tensor_tensor(a, a, -1.0, a, ALU.mult, ALU.max).then_inc(s["ang"], 1)
                    chain.end()

            edge_groups(dve, NG, body)
            dve.wait_ge(s["summed"], EG * NG + 2 * EG)
            nc.vector.tensor_copy(st.tail[:, 0:cols], sums[:, 1, EG - 1, :]).then_inc(s["tail"], 1)

        if weighted:
            @block.sync
            def _(sp):
                def body(g, slot, i):
                    sp.wait_ge(s["weighted"], g + 1)
                    sp.dma_start(V[:, slot, :, :],
                                 st.vj[:, bass.ds(g * EG, EG), :]).then_inc(v_in[slot], 16)
                edge_groups(sp, NG, body)

        if not embed:
            return

        @block.sync
        def _(sp):
            def load(g, slot):
                sp.dma_start(EA[:, slot, :, TD:TD + MD],
                             st.msg.rearrange("(p t) d -> p t d", p=P)[:, bass.ds(g * EG, EG), :]
                             ).then_inc(msg_in[slot], 16)

            def store(g, slot):
                sp.wait_ge(s["e_out"], 4 * g + 4 + 4)
                for c in range(2):
                    sp.dma_start(st.e[c][:, bass.ds(g * EG, EG), :],
                                 EB[:, slot, :, c * P:(c + 1) * P]).then_inc(e_st[slot], 16)

            def load_next_then_store(g, slot):
                sp.wait_ge(s["tposed"], EG * g + EG + 2 * EG)
                load(g + 2, slot)
                store(g, slot)

            def retire(slot, i):
                sp.wait_ge(e_st[slot], 32 * (i + 1))
                sp.sem_inc(s["eb_free"], 1)

            load(0, 0)
            load(1, 1)
            load_next_then_store(0, 0)
            with sp.Fori(0, NG // 2 - 2) as i:
                load_next_then_store(2 * i + 1, 1)
                retire(0, i)
                load_next_then_store(2 * i + 2, 0)
                retire(1, i)
            load_next_then_store(NG - 3, 1)
            retire(0, NG // 2 - 2)
            store(NG - 2, 0)
            retire(1, NG // 2 - 2)
            store(NG - 1, 1)
            retire(0, NG // 2 - 1)
            retire(1, NG // 2 - 1)

        @block.scalar
        def _(act):
            def body(g, slot, i):
                act.wait_ge(s["ang"], g + 3)
                act.wait_ge(s["tposed"], EG * g + EG)
                act.activation(EA[:, slot, :, 0:TD], ang[:, slot, :, :], ACT.Sin, scale=-1.0,
                               bias=st.half_pi[:, 0:1]).then_inc(s["tenc"], 1)
                for half in range(2):
                    n = (4 if half == 0 else EG - 4) * P
                    act.wait_ge(s["tposed"], EG * g + (4 if half == 0 else EG) + 2 * EG)
                    act.wait_ge(s["e_done"], 4 * g + 4)
                    act.activation(eaT[:, slot, half * BANK:half * BANK + n], psA[:, 2 * slot + half, 0:n],
                                   ACT.Copy).then_inc(s["eat"], 1)
                for b in range(4):
                    n = min(2, EG - 2 * b)
                    act.wait_ge(s["e_done"], 4 * g + b + 1 + 8)
                    act.wait_ge(s["eb_free"], g + 1)
                    act.activation(EB[:, slot, 2 * b:2 * b + n, :],
                                   psB[:, b, 0:n * 2 * P].rearrange("p (t d) -> p t d", d=2 * P),
                                   ACT.Copy).then_inc(s["e_out"], 1)
            edge_groups(act, NG, body)

        @block.tensor
        def _(pe):
            def body(g, slot, i):
                pe.wait_ge(s["tenc"], g + 3)
                pe.wait_ge(msg_in[slot], 16 * (i + 1))
                pe.wait_ge(s["eat"], 2 * g + 2)
                for j in range(EG):
                    nc.tensor.transpose(psA[:, 2 * slot + j // 4, (j % 4) * P:(j % 4 + 1) * P],
                                        EA[:, slot, j, :], st.ident[:, :]).then_inc(s["tposed"], 1)
                for b in range(4):
                    if b in (0, 2):
                        pe.wait_ge(s["eat"], 2 * g + b // 2 + 1 + 4)
                    pe.wait_ge(s["e_out"], 4 * g + b + 1)
                    for j in range(2 * b, min(2 * b + 2, EG)):
                        ins = nc.tensor.matmul(psB[:, b, (j % 2) * 2 * P:(j % 2 + 1) * 2 * P],
                                               eaT[:, slot, j * P:(j + 1) * P], st.we[:, :],
                                               start=True, stop=True)
                    ins.then_inc(s["e_done"], 1)
            edge_groups(pe, NG, body)


def carry_phase(nc, st, agg, cols):
    s = fresh_semaphores(nc, st, ["c", "sum"], gpsimd_dma=("got", "put"))
    with ExitStack() as ctx:
        row = ctx.enter_context(nc.sbuf_tensor(f"row_{st.phase}", [P, cols], F32))
        block = ctx.enter_context(nc.Block())

        @block.tensor
        def _(pe):
            nc.tensor.matmul(st.psA[:, 0, 0:cols], st.carry[:, :], st.tail[:, 0:cols],
                             start=True, stop=True).then_inc(s["c"], 1)

        @block.gpsimd
        def _(pool):
            nc.gpsimd.indirect_dma_start(row[:, :], None, agg[:, :],
                                         bass.IndirectOffsetOnAxis(st.carry_from[:, 0:1], 0)
                                         ).then_inc(s["got"], 16)
            pool.wait_ge(s["sum"], 1)
            nc.gpsimd.indirect_dma_start(agg[:, :], bass.IndirectOffsetOnAxis(st.carry_to[:, 0:1], 0),
                                         row[:, :], None, bounds_check=st.NR - 1,
                                         oob_is_err=False).then_inc(s["put"], 16)
            pool.wait_ge(s["put"], 16)

        @block.vector
        def _(dve):
            dve.wait_ge(s["c"], 1)
            dve.wait_ge(s["got"], 16)
            nc.vector.tensor_tensor(row[:, :], row[:, :], st.psA[:, 0, 0:cols], ALU.add).then_inc(s["sum"], 1)


def score_phase(nc, st, conv):
    EC, NG = st.EC, st.EC // EG
    names = ["idx_copied", "fence", "scored", "v_ready", "step", "e0", "e1", "v_st0", "v_st1", "v_free"]
    s = fresh_semaphores(nc, st, names, dict(scored=2, v_ready=2, v_free=2),
                         gpsimd_dma=("got0", "got1"))
    got, e_in, v_st = (s["got0"], s["got1"]), (s["e0"], s["e1"]), (s["v_st0"], s["v_st1"])
    scale = 1.0 / math.sqrt(P // HEADS)
    with ExitStack() as ctx:
        sb = lambda n, sh, d=F32: ctx.enter_context(nc.sbuf_tensor(f"{n}_{st.phase}", sh, d))
        idx = sb("idx", [P, 2, 2, EG], I32)
        KV = sb("KV", [P, 2, EG, 2 * P])
        Q = sb("Q", [P, 2, EG, P])
        Eb = sb("Eb", [P, 2, EG, P])
        V = sb("V", [P, 2, EG, P])
        dots = sb("dots", [P, 2, EG * HEADS])
        block = ctx.enter_context(nc.Block())

        @block.gpsimd
        def _(pool):
            def body(g, slot, i):
                pool.wait_ge(s["scored"], g + 1)
                pool.sem_inc(s["fence"], 1)
                for side, index in ((0, st.src_i), (1, st.qidx_i)):
                    nc.gpsimd.tensor_copy(idx[:, slot, side, :], index[:, bass.ds(g * EG, EG)]
                                          ).then_inc(s["idx_copied"], 1)
                pool.wait_ge(s["idx_copied"], 2 * g + 2)
                pool.sem_inc(s["fence"], 1)
                for j in range(EG):
                    nc.gpsimd.indirect_dma_start(KV[:, slot, j, :], None, st.kv[:, :],
                                                 bass.IndirectOffsetOnAxis(idx[:, slot, 0, j:j + 1], 0)
                                                 ).then_inc(got[slot], 16)
                    nc.gpsimd.indirect_dma_start(Q[:, slot, j, :], None, st.q[:, :],
                                                 bass.IndirectOffsetOnAxis(idx[:, slot, 1, j:j + 1], 0)
                                                 ).then_inc(got[slot], 16)
            edge_groups(pool, NG, body)

        @block.sync
        def _(sp):
            def load(g, slot):
                sp.dma_start(Eb[:, slot, :, :], st.e[conv][:, bass.ds(g * EG, EG), :]).then_inc(e_in[slot], 16)

            def store(g, slot):
                sp.wait_ge(s["v_ready"], g + 3)
                sp.dma_start(st.vj[:, bass.ds(g * EG, EG), :], V[:, slot, :, :]).then_inc(v_st[slot], 16)

            def store_then_load(g, slot):
                store(g, slot)
                sp.wait_ge(s["scored"], g + 3)
                load(g + 2, slot)

            def retire(slot, i):
                sp.wait_ge(v_st[slot], 16 * (i + 1))
                sp.sem_inc(s["v_free"], 1)

            load(0, 0)
            load(1, 1)
            store_then_load(0, 0)
            with sp.Fori(0, NG // 2 - 2) as i:
                store_then_load(2 * i + 1, 1)
                retire(0, i)
                store_then_load(2 * i + 2, 0)
                retire(1, i)
            store_then_load(NG - 3, 1)
            retire(0, NG // 2 - 2)
            store(NG - 2, 0)
            retire(1, NG // 2 - 2)
            store(NG - 1, 1)
            retire(0, NG // 2 - 1)
            retire(1, NG // 2 - 1)

        @block.vector
        def _(dve):
            chain = Steps(s["step"], 3)

            def body(g, slot, i):
                chain.start(g)
                dve.wait_ge(got[slot], 32 * EG * (i + 1))
                dve.wait_ge(e_in[slot], 16 * (i + 1))
                dve.wait_ge(s["v_free"], g + 1)
                nc.vector.tensor_tensor(V[:, slot, :, :], KV[:, slot, :, P:2 * P], Eb[:, slot, :, :],
                                        ALU.add).then_inc(s["v_ready"], 1)
                k = KV[:, slot, :, 0:P]
                chain.mark(nc.vector.tensor_tensor(k, k, Eb[:, slot, :, :], ALU.add))
                chain.wait(dve)
                chain.mark(nc.vector.tensor_tensor(Q[:, slot, :, :], k, Q[:, slot, :, :], ALU.mult))
                chain.wait(dve)
                chain.mark(nc.vector.tensor_reduce(
                    dots[:, slot, :], Q[:, slot, :, :].rearrange("p t (h c) -> p (t h) c", h=HEADS),
                    AX.X, ALU.add))
                chain.wait(dve)
                nc.vector.tensor_scalar(st.alpha[:, :, bass.ds(g * EG, EG)].rearrange("p h t -> p t h"),
                                        dots[:, slot, :].rearrange("p (t h) -> p t h", h=HEADS), scale, None,
                                        ALU.mult).then_inc(s["scored"], 1)
                chain.end()
            edge_groups(dve, NG, body)


def softmax_phase(nc, st):
    EC = st.EC
    s = fresh_semaphores(nc, st, ["step", "d", "m", "e", "x", "t", "u"])
    H = HEADS
    with ExitStack() as ctx:
        sb = lambda n, sh, d=F32: ctx.enter_context(nc.sbuf_tensor(f"{n}_{st.phase}", sh, d))
        fwd = sb("fwd", [P, H, EC])
        seg = sb("seg", [P, H, EC])
        diag = sb("diag", [P, 2 * H, P])
        cand = sb("cand", [P, 2, 2 * H, P])
        top = sb("top", [P, 2, H])
        both = sb("both", [P, 2, 2 * H])
        part = sb("part", [P, 2 * H])
        pen_in = sb("pen_in", [P, 2, EC])
        out_of = sb("out_of", [P, 2, EC])
        block = ctx.enter_context(nc.Block())
        inside = (st.in_first, st.in_last)

        @block.vector
        def _(dve):
            chain = Steps(s["step"], 999)
            chain.start(0)

            def link(ins):
                chain.mark(ins)
                chain.wait(dve)

            for side in range(2):
                link(nc.vector.tensor_scalar(pen_in[:, side, :], inside[side][:, :], BIG, -BIG,
                                             ALU.mult, ALU.add))
                link(nc.vector.tensor_scalar(out_of[:, side, :], inside[side][:, :], -1.0, 1.0,
                                             ALU.mult, ALU.add))
            for h in range(H):
                link(nc.vector.tensor_tensor_scan(fwd[:, h, :], st.pen[:, :], st.alpha[:, h, :], -BIG,
                                                  ALU.add, ALU.max))
                link(nc.vector.tensor_tensor_scan(seg[:, h, ::-1], st.penn[:, ::-1], fwd[:, h, ::-1], -BIG,
                                                  ALU.add, ALU.max))
                link(nc.vector.tensor_scalar(diag[:, h, :], st.ident[:, :], seg[:, h, 0:1], None, ALU.mult))
                link(nc.vector.tensor_scalar(diag[:, H + h, :], st.ident[:, :], seg[:, h, EC - 1:EC], None,
                                             ALU.mult))
            nc.vector.memset(top[:, :, :], 0.0).then_inc(s["d"], 1)
            dve.wait_ge(s["d"], 1)
            dve.wait_ge(s["m"], 1)
            for side in range(2):
                for other in range(2):
                    link(nc.vector.tensor_tensor(
                        cand[:, side, other * H:(other + 1) * H, :],
                        st.psA[:, other, :].rearrange("p (h q) -> p h q", h=H),
                        st.pen_same[:, 2 * side + other, :].unsqueeze(1).broadcast_to([P, H, P]), ALU.add))
                link(nc.vector.tensor_reduce(both[:, side, :], cand[:, side, :, :], AX.X, ALU.max))
                link(nc.vector.tensor_tensor(top[:, side, :], both[:, side, 0:H], both[:, side, H:2 * H],
                                             ALU.max))
            for h in range(H):
                for side in range(2):
                    link(nc.vector.scalar_tensor_tensor(seg[:, h, :], pen_in[:, side, :], top[:, side, h:h + 1],
                                                        seg[:, h, :], ALU.add, ALU.max))
            link(nc.vector.tensor_tensor(st.alpha[:, :, :], st.alpha[:, :, :], seg[:, :, :], ALU.subtract))
            nc.vector.memset(part[:, :], 0.0).then_inc(s["x"], 1)
            dve.wait_ge(s["x"], 1)
            dve.wait_ge(s["e"], 1)
            for h in range(H):
                link(nc.vector.tensor_tensor_scan(fwd[:, h, :], st.cont[:, :], st.alpha[:, h, :], 0.0,
                                                  ALU.mult, ALU.add))
                link(nc.vector.scalar_tensor_tensor(seg[:, h, :], st.contn[:, :], -1.0, fwd[:, h, :],
                                                    ALU.mult, ALU.mult))
                link(nc.vector.tensor_tensor(fwd[:, h, :], fwd[:, h, :], seg[:, h, :], ALU.add))
                link(nc.vector.tensor_tensor_scan(seg[:, h, ::-1], st.contn[:, ::-1], fwd[:, h, ::-1], 0.0,
                                                  ALU.mult, ALU.add))
            link(nc.vector.tensor_scalar(part[:, 0:H], seg[:, :, 0], 1.0, None, ALU.mult))
            link(nc.vector.tensor_scalar(part[:, H:2 * H], seg[:, :, EC - 1], st.two_ended[:, 0:1], None,
                                         ALU.mult))
            nc.vector.memset(both[:, :, :], 0.0).then_inc(s["t"], 1)
            dve.wait_ge(s["t"], 1)
            dve.wait_ge(s["u"], 1)
            link(nc.vector.tensor_copy(top[:, :, :].rearrange("p s h -> p (s h)"), st.psB[:, 0, 0:2 * H]))
            for h in range(H):
                for side in range(2):
                    link(nc.vector.tensor_tensor(seg[:, h, :], seg[:, h, :], out_of[:, side, :], ALU.mult))
                    link(nc.vector.scalar_tensor_tensor(seg[:, h, :], inside[side][:, :], top[:, side, h:h + 1],
                                                        seg[:, h, :], ALU.mult, ALU.add))
            link(nc.vector.tensor_scalar(seg[:, :, :], seg[:, :, :], 1e-16, None, ALU.add))
            link(nc.vector.reciprocal(fwd[:, :, :], seg[:, :, :]))
            link(nc.vector.tensor_tensor(st.alpha[:, :, :], st.alpha[:, :, :], fwd[:, :, :], ALU.mult))

        @block.scalar
        def _(act):
            act.wait_ge(s["x"], 1)
            act.activation(st.alpha[:, :, :], st.alpha[:, :, :], ACT.Exp).then_inc(s["e"], 1)

        @block.tensor
        def _(pe):
            pe.wait_ge(s["d"], 1)
            for side in range(2):
                for h in range(H):
                    ins = nc.tensor.matmul(st.psA[:, side, h * P:(h + 1) * P], st.ones[:, :],
                                           diag[:, side * H + h, :], start=True, stop=True)
            ins.then_inc(s["m"], 1)
            pe.wait_ge(s["t"], 1)
            for side in range(2):
                for other in range(2):
                    mask = st.same[:, 2 * other + side, :]
                    ins = nc.tensor.matmul(st.psB[:, 0, side * H:(side + 1) * H], mask,
                                           part[:, other * H:(other + 1) * H],
                                           start=(other == 0), stop=(other == 1))
            ins.then_inc(s["u"], 1)


def build(nc, a, out):
    st = State()
    st.N, D = a["x"].shape
    st.E = a["src"].shape[0]
    st.MD = a["edge_attr_64"].shape[1]
    st.TD = a["L1_gnn_Wt"].shape[1]
    assert D == P and st.TD + st.MD == P
    st.NGROUPS = -(-st.N // (P * NJ))
    st.NR = st.NGROUPS * P * NJ
    st.TAILP = (st.N - (st.NGROUPS - 1) * P * NJ) // NJ
    st.EC = -(-st.E // (P * 2 * EG)) * 2 * EG
    assert st.TAILP * NJ == st.N - (st.NGROUPS - 1) * P * NJ and st.NGROUPS % 2 == 1
    assert st.E // st.EC == P - 1 and st.NR < NO_NODE and st.NR == P * st.EC
    EC, NR, N = st.EC, st.NR, st.N
    dram = lambda n, sh: nc.dram_tensor(n, sh, F32, kind="Internal").ap()
    st.msg = dram("msg_padded", [P * EC, st.MD])
    table0 = dram("table0", [NR, W0COLS])
    table1, table2 = dram("table1", [NR, P]), dram("table2", [NR, P])
    st.agg0, st.agg = dram("agg0", [NR, W0COLS]), dram("agg", [NR, P])
    x1 = dram("x1", [NR, P])
    st.kv, st.q, st.skip = dram("kv", [NR, 2 * P]), dram("q", [NR, P]), dram("skip", [NR, P])
    skip2 = dram("skip2", [NR, P])
    st.e = [dram(f"edge_emb{c}", [P, EC, P]) for c in range(2)]
    st.vj = dram("vj", [P, EC, P])
    with ExitStack() as ctx:
        sb = lambda n, sh, d=F32: ctx.enter_context(nc.sbuf_tensor(n, sh, d))
        st.src_i, st.sidx_i, st.qidx_i = sb("src_i", [P, EC], I32), sb("sidx_i", [P, EC], I32), sb("qidx_i", [P, EC], I32)
        st.dstf, st.ew, st.rel = sb("dstf", [P, EC]), sb("ew", [P, EC]), sb("rel", [P, EC])
        st.cont, st.contn, st.pen, st.penn = (sb(n, [P, EC]) for n in ("cont", "contn", "pen", "penn"))
        st.in_first, st.in_last = sb("in_first", [P, EC]), sb("in_last", [P, EC])
        st.nv, st.inv = sb("nv", [P, NR // P]), sb("inv_deg", [P, NR // P])
        st.alpha = sb("alpha", [P, HEADS, EC])
        st.ident, st.tri, st.ones = sb("ident", [P, P]), sb("tri", [P, P]), sb("ones", [P, P])
        st.carry = sb("carry", [P, P])
        st.same, st.pen_same = sb("same", [P, 4, P]), sb("pen_same", [P, 4, P])
        st.tail = sb("tail", [P, W0COLS])
        st.two_ended = sb("two_ended", [P, 1])
        st.carry_to, st.carry_from = sb("carry_to", [P, 1], I32), sb("carry_from", [P, 1], I32)
        st.eps, st.half_pi = sb("eps", [P, 1]), sb("half_pi", [P, 1])
        st.w = [sb(f"w{i}", [P, P]) for i in range(3)]
        st.w4, st.b4 = sb("w4", [P, 2, 4 * P]), sb("b4", [P, 2, 4 * P])
        st.we = sb("we", [P, 2 * P])
        st.b0 = sb("b0", [P, 3, P])
        st.gb = sb("gb", [P, 4])
        st.wt, st.bt = sb("wt", [P, st.TD]), sb("bt", [P, st.TD])
        st.psA = ctx.enter_context(nc.psum_tensor("psA", [P, 4, BANK], F32))
        st.psB = ctx.enter_context(nc.psum_tensor("psB", [P, 4, BANK], F32))
        st.pool = [ctx.enter_context(nc.semaphore(f"phase_sem{i}")) for i in range(28)]

        st.phase, st.ctx = 0, ctx

        def run(fn, *args, **kw):
            fn(nc, st, *args, **kw)
            nc.all_engine_barrier()
            st.phase += 1

        run(setup_phase, a)
        run(node_phase, "first", resid=a["x"], w=0, stores=[(table0, 0, W0COLS)], first_table=True)
        run(segment_sum_phase, table0, W0COLS, st.agg0, take_rel=True)
        run(carry_phase, st.agg0, W0COLS)
        run(node_phase, "deg", agg=st.agg0, add=table0, bias=0, w=1, affine=0, stores=[(table1, 0, P)])
        run(segment_sum_phase, table1, P, st.agg, embed=True)
        run(carry_phase, st.agg, P)
        run(node_phase, "sage", agg=st.agg, add=table1, bias=1, w=2, affine=2, stores=[(table2, 0, P)])
        run(segment_sum_phase, table2, P, st.agg)
        run(carry_phase, st.agg, P)
        tables = lambda skip: [(st.kv, 0, 2 * P), (st.q, 2 * P, 3 * P), (skip, 3 * P, 4 * P)]
        run(node_phase, "sage", agg=st.agg, add=table2, resid=a["x"], bias=2, wide=0, stores=tables(st.skip),
            final=x1)
        for conv in range(2):
            run(score_phase, conv)
            run(softmax_phase)
            run(segment_sum_phase, None, P, st.agg, weighted=True)
            run(carry_phase, st.agg, P)
            if conv == 0:
                run(node_phase, "conv", agg=st.agg, add=st.skip, wide=1, stores=tables(skip2))
        run(node_phase, "final", agg=st.agg, add=skip2, resid=x1, final=out)


_INS = ["x", "src", "dst", "edge_attr_64", "edge_weight", "node_vec",
        "L0_gnn_W0", "L0_gnn_b0", "L0_gnn_W1", "L0_gnn_b1", "L0_gnn_W2", "L0_gnn_b2",
        "L0_gnn_g0", "L0_gnn_be0", "L0_gnn_g1", "L0_gnn_be1", "L1_gnn_Wt", "L1_gnn_bt",
        "L1_gnn_Wq1", "L1_gnn_bq1", "L1_gnn_Wk1", "L1_gnn_bk1", "L1_gnn_Wv1", "L1_gnn_bv1", "L1_gnn_We1",
        "L1_gnn_Wskip1", "L1_gnn_bskip1", "L1_gnn_Wq2", "L1_gnn_bq2", "L1_gnn_Wk2", "L1_gnn_bk2",
        "L1_gnn_Wv2", "L1_gnn_bv2", "L1_gnn_We2", "L1_gnn_Wskip2", "L1_gnn_bskip2"]


def kernel(**inputs):
    import numpy as _np
    import concourse.bacc as _bacc
    from concourse import mybir as _mybir
    from concourse.bass_utils import run_bass_kernel_spmd as _run

    nc = _bacc.Bacc("TRN2", target_bir_lowering=False, num_devices=1)
    arrays, args = {}, {}
    for name in _INS:
        arr = _np.ascontiguousarray(inputs[name])
        arrays[f"in_{name}"] = arr
        args[name] = nc.dram_tensor(f"in_{name}", arr.shape, _mybir.dt.from_np(arr.dtype), kind="ExternalInput").ap()
    out = nc.dram_tensor("out_0", inputs["x"].shape, F32, kind="ExternalOutput").ap()
    build(nc, args, out)
    r = _run(nc, [arrays], core_ids=[0])
    return r.results[0]["out_0"]
```

```python
import math
from contextlib import ExitStack

import concourse.bass as bass
from concourse import mybir

F32 = mybir.dt.float32
BF16 = mybir.dt.bfloat16
I32 = mybir.dt.int32
U32 = mybir.dt.uint32
ALU = mybir.AluOpType
ACT = mybir.ActivationFunctionType
AX = mybir.AxisListType

P = 128
NJ = 8
EG = 7
HALF = NJ // 2
BANK = 512
HEADS = 4
EPS = 1e-5
W0COLS = 132
BIG = 1.0e38
ZRING = 4
ZPARTS = 28
MPARTS = 25
NO_NODE = 65536
MAGIC = 1.5 * 2.0 ** 23
TWO_PI_HI = 6.28125
TWO_PI_LO = 2.0 * math.pi - TWO_PI_HI


class Steps:

    def __init__(self, sem, per_group):
        self.sem, self.per_group = sem, per_group

    def start(self, g):
        self.g, self.k = g, 0

    def mark(self, ins):
        ins.then_inc(self.sem, 1)
        self.k += 1

    def wait(self, eng):
        eng.wait_ge(self.sem, self.g * self.per_group + self.k)

    def end(self):
        assert self.k == self.per_group, (self.k, self.per_group)


class State:
    pass


def fresh_semaphores(nc, st, names, primed=None, gpsimd_dma=()):
    assert len(names) <= len(st.pool)
    nc.gpsimd.sem_clear(range(st.pool[0].num, st.pool[-1].num + 1))
    sems = dict(zip(names, st.pool))
    for name, credit in (primed or {}).items():
        nc.gpsimd.sem_inc(sems[name], credit)
    nc.all_engine_barrier()
    for name in gpsimd_dma:
        sems[name] = st.ctx.enter_context(nc.semaphore(f"{name}_{st.phase}"))
    return sems


def setup_phase(nc, st, a):
    N, E, EC, NR = st.N, st.E, st.EC, st.NR
    full = E // EC
    rest = E - full * EC
    s = fresh_semaphores(nc, st, ["fill", "load", "load2", "step", "diag", "bc", "diag2", "tri"])
    with ExitStack() as ctx:
        sb = lambda n, sh, d=F32: ctx.enter_context(nc.sbuf_tensor(n, sh, d))
        dst_i = sb("dst_i", [P, EC], I32)
        zeros = st.zeros
        next_i = sb("next_i", [P, 1], I32)
        nextf = sb("nextf", [P, 1])
        lastf = sb("lastf", [P, EC])
        tmp = sb("tmp", [P, EC])
        diag = sb("diag", [P, 2, P])
        ends = sb("ends", [P, 4])
        bits = sb("bits", [3, 3, 11 * P], BF16)
        left = sb("left", [3, 11 * P])
        block = ctx.enter_context(nc.Block())
        n_w = 0

        @block.gpsimd
        def _(pool):
            nc.gpsimd.memset(zeros[:, :], 0.0).then_inc(s["fill"], 1)
            nc.gpsimd.memset(st.src_i[:, :], 0).then_inc(s["fill"], 1)
            nc.gpsimd.memset(dst_i[:, :], NO_NODE).then_inc(s["fill"], 1)
            nc.gpsimd.memset(next_i[:, :], NO_NODE + 1).then_inc(s["fill"], 1)
            nc.gpsimd.memset(st.ew[:, :], 0.0).then_inc(s["fill"], 1)
            nc.gpsimd.memset(st.nv[:, :], 0.0).then_inc(s["fill"], 1)
            nc.gpsimd.memset(st.ident[:, :], 0.0).then_inc(s["fill"], 1)
            nc.gpsimd.memset(st.tri[:, :], 1.0).then_inc(s["fill"], 1)
            nc.gpsimd.memset(st.ones[:, :], 1.0).then_inc(s["fill"], 1)
            nc.gpsimd.memset(st.eps[:, :], EPS).then_inc(s["fill"], 1)
            nc.gpsimd.memset(st.half_pi[:, :], math.pi / 2).then_inc(s["fill"], 1)
            pool.wait_ge(s["fill"], 11)
            nc.gpsimd.affine_select(out=st.ident[:, :], in_=st.ident[:, :], compare_op=ALU.not_equal, fill=1.0,
                                    base=0, pattern=[[-1, P]], channel_multiplier=1).then_inc(s["tri"], 1)
            nc.gpsimd.affine_select(out=st.tri[:, :], in_=st.tri[:, :], compare_op=ALU.is_gt, fill=0.0,
                                    base=0, pattern=[[1, P]], channel_multiplier=-1).then_inc(s["tri"], 1)

        @block.sync
        def _(sp):
            nonlocal n_w
            plain = [(st.w[0], a["L0_gnn_W0"]), (st.w[1], a["L0_gnn_W1"]), (st.w[2], a["L0_gnn_W2"])]
            for c in range(2):
                for j, name in enumerate(("Wk", "Wv", "Wq", "Wskip")):
                    plain.append((st.w4[:, c, j * P:(j + 1) * P], a[f"L1_gnn_{name}{c + 1}"]))
                    bias = a[f"L1_gnn_b{name[1:]}{c + 1}"]
                    plain.append((st.b4[:, c, j * P:(j + 1) * P],
                                  bias.rearrange("(o n) -> o n", o=1).broadcast_to([P, P])))
                plain.append((st.we[:, c * P:(c + 1) * P], a[f"L1_gnn_We{c + 1}"]))
            for layer in range(3):
                plain.append((st.b0[:, layer, :],
                              a[f"L0_gnn_b{layer}"].rearrange("(o n) -> o n", o=1).broadcast_to([P, P])))
            for j, name in enumerate(("g0", "be0", "g1", "be1")):
                plain.append((st.gb[:, j:j + 1], a[f"L0_gnn_{name}"].rearrange("(n o) -> n o", o=1)))
            TD = st.TD
            plain.append((st.wt[:, :], a["L1_gnn_Wt"].broadcast_to([P, TD])))
            plain.append((st.bt[:, :], a["L1_gnn_bt"].rearrange("(o n) -> o n", o=1).broadcast_to([P, TD])))
            for dst, src in plain:
                sp.dma_start(dst if isinstance(dst, bass.AP) else dst[:, :], src).then_inc(s["load"], 16)
            n_w = st.n_plain = len(plain)
            sp.wait_ge(s["fill"], 11)
            edge_lists = [(st.src_i, a["src"]), (dst_i, a["dst"]), (st.ew, a["edge_weight"])]
            for tile, flat in edge_lists:
                sp.dma_start(tile[0:full, :],
                             flat[0:full * EC].rearrange("(p t) -> p t", t=EC)).then_inc(s["load2"], 16)
                sp.dma_start(tile[full:full + 1, 0:rest],
                             flat[full * EC:E].rearrange("(o t) -> o t", o=1)).then_inc(s["load2"], 16)
            with nc.allow_non_contiguous_dma(reason="one element per partition"):
                sp.dma_start(next_i[0:full, :],
                             a["dst"][EC:EC + (full - 1) * EC + 1:EC].rearrange("(p o) -> p o", o=1)
                             ).then_inc(s["load2"], 16)
            G, tail = st.NGROUPS - 1, st.TAILP
            nvv = st.nv[:, :].rearrange("p (g j) -> p g j", j=NJ)
            sp.dma_start(nvv[:, 0:G, :],
                         a["node_vec"][0:G * P * NJ].rearrange("(g p j) -> p g j", p=P, j=NJ)
                         ).then_inc(s["load2"], 16)
            sp.dma_start(nvv[0:tail, G, :],
                         a["node_vec"][G * P * NJ:N].rearrange("(p j) -> p j", j=NJ)).then_inc(s["load2"], 16)
            sp.wait_ge(s["load"], 16 * n_w)
            sp.wait_ge(s["load2"], 16 * 9)

        @block.scalar
        def _(act):
            act.wait_ge(s["fill"], 11)
            pad = (P * EC - E) * st.MD // 16
            act.dma_start(st.msg[E:P * EC, :].rearrange("(p r) d -> p (r d)", p=16),
                          zeros[0:16, 0:pad]).then_inc(st.filled, 16)

        @block.vector
        def _(dve):
            chain = Steps(s["step"], 99)
            chain.start(0)

            def link(ins):
                chain.mark(ins)
                chain.wait(dve)

            dve.wait_ge(s["load2"], 16 * 9)
            dve.wait_ge(s["load"], 16 * st.n_plain)
            link(nc.vector.tensor_copy(st.dstf[:, :], dst_i[:, :]))
            link(nc.vector.tensor_copy(nextf[:, :], next_i[:, :]))
            link(nc.vector.memset(st.cont[:, 0:1], 0.0))
            link(nc.vector.tensor_tensor(st.cont[:, 1:EC], st.dstf[:, 1:EC], st.dstf[:, 0:EC - 1], ALU.is_equal))
            link(nc.vector.memset(st.contn[:, EC - 1:EC], 0.0))
            link(nc.vector.tensor_scalar(st.contn[:, 0:EC - 1], st.cont[:, 1:EC], 1.0, None, ALU.mult))
            link(nc.vector.tensor_tensor(lastf[:, 0:EC - 1], st.dstf[:, 0:EC - 1], st.dstf[:, 1:EC], ALU.not_equal))
            link(nc.vector.tensor_tensor(lastf[:, EC - 1:EC], st.dstf[:, EC - 1:EC], nextf[:, :], ALU.not_equal))
            link(nc.vector.tensor_scalar(tmp[:, :], lastf[:, :], -float(NO_NODE), float(NO_NODE),
                                         ALU.mult, ALU.add))
            link(nc.vector.tensor_tensor(tmp[:, :], tmp[:, :], st.dstf[:, :], ALU.add))
            link(nc.vector.tensor_copy(st.sidx_i[:, :], tmp[:, :]))
            link(nc.vector.tensor_scalar(tmp[:, :], st.dstf[:, :], float(N - 1), None, ALU.min))
            link(nc.vector.tensor_copy(st.qidx_i[:, :], tmp[:, :]))
            link(nc.vector.tensor_scalar(st.pen[:, :], st.cont[:, :], BIG, -BIG, ALU.mult, ALU.add))
            link(nc.vector.tensor_scalar(st.penn[:, :], st.contn[:, :], BIG, -BIG, ALU.mult, ALU.add))
            first, last = st.dstf[:, 0:1], st.dstf[:, EC - 1:EC]
            link(nc.vector.tensor_scalar(st.in_first[:, :], st.dstf[:, :], first, None, ALU.is_equal))
            link(nc.vector.tensor_scalar(st.in_last[:, :], st.dstf[:, :], last, None, ALU.is_equal))
            link(nc.vector.tensor_tensor(ends[:, 0:1], first, last, ALU.not_equal))
            link(nc.vector.tensor_scalar(st.two_ended[:, :], ends[:, 0:1], 1.0, None, ALU.mult))
            link(nc.vector.tensor_tensor(ends[:, 1:2], ends[:, 0:1], lastf[:, EC - 1:EC], ALU.max))
            link(nc.vector.tensor_scalar(ends[:, 2:3], ends[:, 1:2], -float(NO_NODE), float(NO_NODE),
                                         ALU.mult, ALU.add))
            link(nc.vector.tensor_tensor(ends[:, 3:4], ends[:, 2:3], first, ALU.add))
            link(nc.vector.tensor_copy(st.carry_to[:, :], ends[:, 3:4]))
            link(nc.vector.tensor_copy(st.carry_from[:, :], first))
            dve.wait_ge(s["tri"], 2)
            link(nc.vector.tensor_scalar(diag[:, 0, :], st.ident[:, :], first, None, ALU.mult))
            chain.mark(nc.vector.tensor_scalar(diag[:, 1, :], st.ident[:, :], last, None, ALU.mult))
            dve.sem_inc(s["diag2"], 1)
            chain.wait(dve)
            nc.vector.memset(ends[:, 0:1], 0.0).then_inc(s["diag"], 1)
            dve.wait_ge(s["bc"], 1)
            for m, (row, col) in enumerate(((0, first), (1, first), (0, last), (1, last))):
                link(nc.vector.tensor_scalar(st.same[:, m, :], st.psA[:, 0, row * P:(row + 1) * P], col, None,
                                             ALU.is_equal))
            link(nc.vector.tensor_tensor(st.carry[:, :], st.same[:, 2, :], st.tri[:, :], ALU.mult))
            k3 = slice(0, 3)
            part = lambda m: bits[k3, m, :]
            whole = st.biases[k3, :]
            link(nc.vector.tensor_copy(part(0), whole))
            link(nc.vector.tensor_tensor(left[k3, :], whole, part(0), ALU.subtract))
            link(nc.vector.tensor_copy(part(1), left[k3, :]))
            link(nc.vector.tensor_tensor(left[k3, :], left[k3, :], part(1), ALU.subtract))
            link(nc.vector.tensor_copy(part(2), left[k3, :]))
            b3 = st.biases3[k3, :]
            link(nc.vector.tensor_scalar(b3, part(0), st.ident[k3, 0:1], None, ALU.mult))
            for m in (1, 2):
                link(nc.vector.scalar_tensor_tensor(b3, part(m), st.ident[k3, m:m + 1], b3, ALU.mult, ALU.add))
            link(nc.vector.memset(st.ones3[:, :], 1.0))
            link(nc.vector.tensor_scalar(st.pen_same[:, :, :], st.same[:, :, :], BIG, -BIG, ALU.mult, ALU.add))

        @block.tensor
        def _(pe):
            pe.wait_ge(s["diag"], 1)
            nc.tensor.matmul(st.psA[:, 0, 0:P], st.ones[:, :], diag[:, 0, :], start=True, stop=True)
            nc.tensor.matmul(st.psA[:, 0, P:2 * P], st.ones[:, :], diag[:, 1, :],
                             start=True, stop=True).then_inc(s["bc"], 1)


def zero_part(st, eng, table, width, k):
    view = table[:, :].rearrange("(p c) d -> p (c d)", p=P)
    piece = st.EC * width // ZPARTS
    eng.dma_start(view[:, k * piece:(k + 1) * piece], st.zeros[:, 0:piece]).then_inc(st.filled, 16)


def message_part(st, eng, k):
    piece = st.E // 16 // MPARTS * st.MD
    rows = lambda t: t.rearrange("(p r) d -> p (r d)", p=16)[:, k * piece:(k + 1) * piece]
    eng.dma_start(rows(st.msg[0:st.E, :]), rows(st.edge_attr), max_dma_last_dim=32768).then_inc(st.filled, 16)


def pipelined(eng, groups, stages, hi=None):
    deepest = max(lag for _, lag in stages)
    lo = -(-deepest // ZRING)
    hi = (groups if hi is None else hi) // ZRING

    def step(k):
        for body, lag in stages:
            if 0 <= k - lag < groups:
                body(k - lag, (k - lag) % 2, (k - lag) // 2, (k - lag) % ZRING)

    for k in range(ZRING * lo):
        step(k)
    with eng.Fori(lo, hi) as turn:
        for c in range(ZRING):
            for body, lag in stages:
                d = c - lag
                body(ZRING * turn + d, d % 2, (ZRING // 2) * turn + d // 2, d % ZRING)
    for k in range(ZRING * hi, groups + deepest):
        step(k)


def node_phase(nc, st, kind, agg=None, add=None, resid=None, bias=None, w=None, wide=None, affine=None,
               stores=(), final=None, first_table=False):
    N, NR, G = st.N, st.NR, st.NGROUPS - 1
    norm = kind in ("first", "deg", "sage")
    sage = kind in ("deg", "sage")
    first = kind == "first"
    nload = 1 if first else 2
    wide_n = wide is not None
    split = wide_n and not norm
    units = NJ if wide_n else NJ // HALF
    ocols = BANK if wide_n else (W0COLS if first_table else P)
    names = ["loaded0", "loaded1", "resid0", "resid1", "deg_in", "z_ready", "step", "stats", "std", "normed",
             "tposed", "h_ready", "y_done",
             "y_out", "nv_put", "stored0", "stored1", "z_out", "z_stored0", "z_stored1", "ones",
             "fence", "o_free", "z_free", "step_b", "inv_step", "y_out_odd", "z_sum"]
    nst = len(stores)
    primed = dict(z_ready=2, normed=ZRING * NJ, tposed=2 * NJ, h_ready=4, y_done=2 * units,
                  y_out=2 if split else 4, y_out_odd=2, o_free=2, z_free=ZRING)
    s = fresh_semaphores(nc, st, names, primed)
    loaded, resid_in = (s["loaded0"], s["loaded1"]), (s["resid0"], s["resid1"])
    stored = (s["stored0"], s["stored1"])
    z_stored = (s["z_stored0"], s["z_stored1"])
    acols = W0COLS if kind == "deg" else P
    ycols = W0COLS if kind == "deg" else P
    grouped = lambda t: t.rearrange("(g p j) d -> p g j d", p=P, j=NJ)

    with ExitStack() as ctx:
        sb = lambda n, sh, d=F32: ctx.enter_context(nc.sbuf_tensor(f"{n}_{st.phase}", sh, d))
        A = sb("A", [P, 2, NJ, acols]) if agg is not None else None
        Y = sb("Y", [P, 2, NJ, ycols]) if add is not None else None
        X = sb("X", [P, 2, NJ, P]) if resid is not None else None
        Z = sb("Z", [P, ZRING, NJ, P])
        ns = lambda slot, zs: slot if norm else zs
        nrm = sb("nrm", [P, 2, NJ, P]) if norm else Z
        bn = sb("bn", [P, 2, NJ, 6])
        mv = sb("mv", [P, 2, NJ, 2])
        std = sb("std", [P, 2, NJ])
        rstd = sb("rstd", [P, 2, NJ])
        deg, deg1 = sb("deg", [P, 2, NJ]), sb("deg1", [P, 2, NJ])
        inv = sb("inv", [P, 2, NJ])
        hT = sb("hT", [P, 2, NJ * P]) if kind != "final" else None
        O = sb("O", [P, 2, NJ, ocols]) if kind != "final" else None
        psA, psB = st.psA, st.psB
        block = ctx.enter_context(nc.Block())

        summands = [(X, resid)] if first else [(A, agg), (Y, add)]

        def load(sp, g, slot, tail, tensors, sems):
            for tile, table in tensors:
                if table.shape[0] == N and tail:
                    src = table[G * P * NJ:N, :].rearrange("(p j) d -> p j d", j=NJ)
                    sp.dma_start(tile[0:st.TAILP, slot, :, :], src).then_inc(sems[slot], 16)
                else:
                    src = grouped(table[0:G * P * NJ, :]) if table.shape[0] == N else grouped(table)
                    sp.dma_start(tile[:, slot:slot + 1, :, :].rearrange("p g j d -> p g (j d)"),
                                 src[:, bass.ds(g, 1), :, :].rearrange("p g j d -> p g (j d)")
                                 ).then_inc(sems[slot], 16)

        @block.sync
        def _(sp):
            def z_out(g, slot, i, zs):
                sp.wait_ge(s["z_out"], g + 1)
                if final.shape[0] == N and isinstance(g, int) and g == G:
                    sp.dma_start(final[G * P * NJ:N, :].rearrange("(p j) d -> p j d", j=NJ),
                                 Z[0:st.TAILP, zs, :, :]).then_inc(z_stored[slot], 16)
                else:
                    dst = grouped(final[0:G * P * NJ, :]) if final.shape[0] == N else grouped(final)
                    sp.dma_start(dst[:, bass.ds(g, 1), :, :].rearrange("p g j d -> p g (j d)"),
                                 Z[:, zs:zs + 1, :, :].rearrange("p g j d -> p g (j d)")
                                 ).then_inc(z_stored[slot], 16)

            def z_retire(g, slot, i, zs):
                sp.wait_ge(z_stored[slot], 16 * (i + 1))
                sp.sem_inc(s["z_free"], 1)

            def load_next(g, slot, i, zs):
                if isinstance(g, int) and g + 2 > G:
                    return
                if sage:
                    sp.wait_ge(s["z_sum"], g + 1)
                    if kind == "deg":
                        sp.wait_ge(s["deg_in"], g + 1)
                else:
                    sp.wait_ge(s["z_ready"], g + 3)
                load(sp, g + 2, slot, isinstance(g, int) and g + 2 == G, summands, loaded)

            def load_next_resid(g, slot, i, zs):
                if isinstance(g, int) and g + 2 > G:
                    return
                sp.wait_ge(s["z_out"], g + 1)
                load(sp, g + 2, slot, isinstance(g, int) and g + 2 == G, [(X, resid)], resid_in)

            def y_out(g, slot, i, zs):
                if split:
                    sp.wait_ge(s["y_out"], (g + 1) * (units // 2) + 2)
                    sp.wait_ge(s["y_out_odd"], (g + 1) * (units // 2) + 2)
                else:
                    sp.wait_ge(s["y_out"], (g + 1) * units + 4)
                if first_table:
                    sp.wait_ge(s["nv_put"], g + 1)
                for table, lo, hi in stores:
                    sp.dma_start(grouped(table)[:, bass.ds(g, 1), :, :].rearrange("p g j d -> p (g j) d"),
                                 O[:, slot, :, lo:hi]).then_inc(stored[slot], 16)

            def zero_agg0(g, slot, i, zs):
                sp.dma_start(grouped(st.agg0)[:, bass.ds(g, 1), :, :].rearrange("p g j d -> p g (j d)"),
                             st.zeros[:, 0:NJ * W0COLS].unsqueeze(1)).then_inc(st.filled, 16)

            def y_retire(g, slot, i, zs):
                sp.wait_ge(stored[slot], 16 * nst * (i + 1))
                sp.sem_inc(s["o_free"], 1)

            for g in range(2):
                load(sp, g, g, False, summands, loaded)
                if final is not None:
                    load(sp, g, g, False, [(X, resid)], resid_in)
            stages = [(load_next, 0)]
            if final is not None:
                stages += [(z_retire, 3), (z_out, 1), (load_next_resid, 1)]
            if kind == "final":
                stages = [(z_retire, 2), (z_out, 0), (load_next, 0), (load_next_resid, 0)]
            if nst:
                lag = 2 if kind == "conv" else 4
                stages += [(y_out, lag), (y_retire, lag + 1)]
            if first_table:
                stages.append((zero_agg0, 0))
            pipelined(sp, G + 1, stages, hi=G - 2)
            if first_table:
                sp.wait_ge(st.filled, 16 * (G + 2))

        @block.gpsimd
        def _(pool):
            def body(g, slot, i, zs):
                pool.wait_ge(loaded[slot], 16 * nload * (i + 1))
                if norm:
                    pool.wait_ge(s["normed"], g * NJ + NJ)
                    if final is not None:
                        pool.wait_ge(s["z_free"], g + 1)
                elif kind == "conv":
                    pool.wait_ge(s["tposed"], g * NJ + NJ)
                else:
                    pool.wait_ge(s["z_free"], g + 1)
                if kind == "first":
                    pool.sem_inc(s["fence"], 1)
                    ins = nc.gpsimd.tensor_copy(Z[:, zs, :, :], X[:, slot, :, :])
                else:
                    if kind == "deg":
                        pool.sem_inc(s["fence"], 1)
                        nc.gpsimd.tensor_copy(deg[:, slot, :], A[:, slot, :, P + 1]).then_inc(s["deg_in"], 1)
                    ins = nc.gpsimd.tensor_tensor(Z[:, zs, :, :], A[:, slot, :, 0:P], Y[:, slot, :, 0:P], ALU.add)
                ins.then_inc(s["z_sum" if sage else "z_ready"], 1)

            def scaled(g, slot, i, zs):
                pool.wait_ge(s["z_sum"], g + 1)
                if kind == "deg":
                    pool.wait_ge(s["inv_step"], 3 * g + 3)
                pool.sem_inc(s["fence"], 1)
                nc.gpsimd.tensor_tensor(
                    Z[:, zs, :, :], Z[:, zs, :, :],
                    st.inv[:, bass.ds(g * NJ, NJ)].unsqueeze(2).broadcast_to([P, NJ, P]),
                    ALU.mult).then_inc(s["z_ready"], 1)

            pipelined(pool, G + 1, [(body, 0)] + ([(scaled, 1 if kind == "deg" else 0)] if sage else []))

        @block.vector
        def _(dve):
            if first_table:
                for slot in range(2):
                    nc.vector.memset(O[:, slot, :, P + 1:W0COLS], 1.0).then_inc(s["ones"], 1)
                dve.wait_ge(s["ones"], 2)
            chain = Steps(s["step"], 2 * NJ - 1 if norm else 0)
            chain_b = Steps(s["step_b"], 1)
            chain_inv = Steps(s["inv_step"], 3)

            def inverse(g, slot, i, zs):
                chain_inv.start(g)
                dve.wait_ge(s["deg_in"], g + 1)
                chain_inv.mark(nc.vector.tensor_scalar(deg1[:, slot, :], deg[:, slot, :], 1.0, None, ALU.add))
                chain_inv.wait(dve)
                chain_inv.mark(nc.vector.reciprocal(inv[:, slot, :], deg1[:, slot, :]))
                chain_inv.wait(dve)
                chain_inv.mark(nc.vector.tensor_scalar(st.inv[:, bass.ds(g * NJ, NJ)], inv[:, slot, :], 1.0, None,
                                                       ALU.mult))
                chain_inv.end()

            def statistics(g, slot, i, zs):
                chain.start(g)
                z = Z[:, zs, :, :]
                dve.wait_ge(s["z_ready"], g + 3)
                if resid is not None and kind != "first":
                    dve.wait_ge(resid_in[slot], 16 * (i + 1))
                    nc.vector.tensor_tensor(z, z, X[:, slot, :, :], ALU.add).then_inc(s["z_out"], 1)
                    dve.wait_ge(s["z_out"], g + 1)
                if norm:
                    for j in range(NJ):
                        chain.mark(nc.vector.bn_stats(bn[:, slot, j, :], Z[:, zs, j, :]))
                    chain.wait(dve)
                    dve.sem_inc(s["fence"], 1)
                    for j in range(NJ):
                        ins = nc.vector.bn_aggr(mv[:, slot, j, :], bn[:, slot, j, :])
                        if j < NJ - 1:
                            chain.mark(ins)
                    ins.then_inc(s["stats"], 1)
                    chain.wait(dve)
                chain.end()

            def normalise(g, slot, i, zs):
                chain_b.start(g)
                dve.wait_ge(s["std"], g + 1)
                chain_b.mark(nc.vector.reciprocal(rstd[:, slot, :], std[:, slot, :]))
                chain_b.wait(dve)
                dve.wait_ge(s["tposed"], g * NJ + NJ)
                for j in range(NJ):
                    nc.vector.tensor_scalar(nrm[:, slot, j, :], Z[:, zs, j, :], mv[:, slot, j, 0:1],
                                            rstd[:, slot, j:j + 1], ALU.subtract,
                                            ALU.mult).then_inc(s["normed"], 1)

            def products_out(g, slot, i, zs):
                dve.wait_ge(s["o_free"], g + 1)
                for u in range(0, units, 2):
                    dve.wait_ge(s["y_done"], g * units + u + 1 + 2 * units)
                    nc.vector.tensor_tensor(O[:, slot, u, :], psB[:, u % 4, :], st.b4[:, wide, :],
                                            ALU.add).then_inc(s["y_out"], 1)

            def node_vec_out(g, slot, i, zs):
                dve.wait_ge(s["o_free"], g + 1)
                nc.vector.tensor_scalar(O[:, slot, :, P], st.nv[:, bass.ds(g * NJ, NJ)], 1.0, None,
                                        ALU.mult).then_inc(s["nv_put"], 1)

            late = 1 if kind == "deg" else 0
            stages = [(statistics, late)] if norm or kind == "final" else []
            if norm:
                stages.insert(0 if kind == "first" else 1, (normalise, 1 + late))
            if kind == "deg":
                stages.insert(0, (inverse, 0))
            if first_table:
                stages.append((node_vec_out, 2))
            if split:
                stages.append((products_out, 0))
            pipelined(dve, G + 1, stages)

        if kind == "final":
            return

        @block.scalar
        def _(act):
            def deviation(g, slot, i, zs):
                act.wait_ge(s["stats"], g + 1)
                act.activation(std[:, slot, :], mv[:, slot, :, 1], ACT.Sqrt,
                               bias=st.eps[:, 0:1]).then_inc(s["std"], 1)

            def features(g, slot, i, zs):
                for half in range(2):
                    act.wait_ge(s["tposed"], g * NJ + (half + 1) * HALF + 2 * NJ)
                    act.wait_ge(s["y_done"], g * units + units)
                    out = hT[:, slot, half * BANK:(half + 1) * BANK]
                    src = psA[:, 2 * slot + half, :]
                    if kind == "conv":
                        ins = act.activation(out, src, ACT.Copy)
                    elif affine is None:
                        ins = act.activation(out, src, ACT.Relu)
                    else:
                        ins = act.activation(out, src, ACT.Relu, scale=st.gb[:, affine:affine + 1],
                                             bias=st.gb[:, affine + 1:affine + 2])
                    ins.then_inc(s["h_ready"], 1)

            def products_out(g, slot, i, zs):
                act.wait_ge(s["o_free"], g + 1)
                for u in range(units):
                    act.wait_ge(s["y_done"], g * units + u + 1 + 2 * units)
                    act.activation(O[:, slot, HALF * u:HALF * (u + 1), 0:P],
                                   psB[:, 2 * slot + u, :].rearrange("p (j d) -> p j d", d=P),
                                   ACT.Copy).then_inc(s["y_out"], 1)

            def wide_products_out(g, slot, i, zs):
                act.wait_ge(s["o_free"], g + 1)
                for u in range(units):
                    act.wait_ge(s["y_done"], g * units + u + 1 + 2 * units)
                    act.activation(O[:, slot, u, :], psB[:, u % 4, :], ACT.Copy).then_inc(s["y_out"], 1)

            def odd_products_out(g, slot, i, zs):
                act.wait_ge(s["o_free"], g + 1)
                for u in range(1, units, 2):
                    act.wait_ge(s["y_done"], g * units + u + 1 + 2 * units)
                    act.activation(O[:, slot, u, :], psB[:, u % 4, :], ACT.Copy).then_inc(s["y_out_odd"], 1)

            stages = [(deviation, 0), (features, 1)] if norm else [(features, 0)]
            if split:
                stages.append((odd_products_out, 1))
            else:
                stages.append((wide_products_out if wide_n else products_out, 2))
            pipelined(act, G + 1, stages)

        @block.tensor
        def _(pe):
            def transposes(g, slot, i, zs):
                if norm:
                    pe.wait_ge(s["normed"], g * NJ + NJ + ZRING * NJ)
                else:
                    pe.wait_ge(s["z_ready"], g + 3)
                pe.wait_ge(s["h_ready"], g * 2 + 2)
                for j in range(NJ):
                    nc.tensor.transpose(psA[:, 2 * slot + j // HALF, (j % HALF) * P:(j % HALF + 1) * P],
                                        nrm[:, ns(slot, zs), j, :], st.ident[:, :]).then_inc(s["tposed"], 1)

            def products(g, slot, i, zs):
                for u in range(units):
                    if u % (units // 2) == 0:
                        pe.wait_ge(s["h_ready"], g * 2 + u // (units // 2) + 1 + 4)
                    if split:
                        pe.wait_ge(s["y_out_odd" if u % 2 else "y_out"], g * (units // 2) + u // 2 + 1)
                    else:
                        pe.wait_ge(s["y_out"], g * units + u + 1)
                    if wide_n:
                        bias_here = u % 2 == 1 or not split
                        ins = nc.tensor.matmul(psB[:, u % 4, :], hT[:, slot, u * P:(u + 1) * P],
                                               st.w4[:, wide, :], start=True, stop=not bias_here)
                        if bias_here:
                            ins = nc.tensor.matmul(psB[:, u % 4, :], st.ones3[:, :], st.bias3[:, wide, :],
                                                   start=False, stop=True)
                    else:
                        for j in range(HALF):
                            t = u * HALF + j
                            nc.tensor.matmul(psB[:, 2 * slot + u, j * P:(j + 1) * P],
                                                   hT[:, slot, t * P:(t + 1) * P], st.w[w][:, :],
                                                   start=True, stop=False)
                            ins = nc.tensor.matmul(psB[:, 2 * slot + u, j * P:(j + 1) * P],
                                                   st.ones3[:, :], st.bias3_sage[:, bias, :],
                                                   start=False, stop=True)
                    ins.then_inc(s["y_done"], 1)

            pipelined(pe, G + 1, [(transposes, 0), (products, 1)])


def edge_groups(eng, total, body):
    with eng.Fori(0, total // 2) as i:
        for slot in range(2):
            body(2 * i + slot, slot, i)


def segment_sum_phase(nc, st, table, cols, agg, embed=False, take_rel=False, weighted=None):
    EC, NG = st.EC, st.EC // EG
    TD, MD = st.TD, st.MD
    names = ["idx_copied", "sidx_copied", "fence", "summed", "rel", "start",
             "msg0", "msg1", "step", "ang", "tenc", "tposed", "eat", "e_done", "e_out", "e_st0", "e_st1",
             "v0", "v1", "weighted", "tail",
             "sums_free", "eb_free"]
    primed = dict(summed=2 * EG, sums_free=2, rel=2, weighted=2, tenc=2, ang=2, tposed=2 * EG,
                  eat=4, e_done=8, e_out=4, eb_free=2)
    s = fresh_semaphores(nc, st, names, primed, gpsimd_dma=("rows0", "rows1", "scat0", "scat1"))
    rows_in, scat = (s["rows0"], s["rows1"]), (s["scat0"], s["scat1"])
    msg_in, e_st, v_in = (s["msg0"], s["msg1"]), (s["e_st0"], s["e_st1"]), (s["v0"], s["v1"])
    with ExitStack() as ctx:
        sb = lambda n, sh, d=F32: ctx.enter_context(nc.sbuf_tensor(f"{n}_{st.phase}", sh, d))
        gidx = sb("gidx", [P, 2, EG], I32)
        sidx = sb("sidx", [P, 2, EG], I32)
        rows = sb("rows", [P, 2, EG, cols])
        sums = sb("sums", [P, 2, EG, cols])
        V = sb("V", [P, 2, EG, P]) if weighted else None
        if embed:
            EA = sb("EA", [P, 2, EG, TD + MD])
            ang = sb("ang", [P, 2, EG, TD])
            turn = sb("turn", [P, EG, TD])
            eaT = sb("eaT", [P, 2, EG * P])
            EB = sb("EB", [P, 2, EG, 2 * P])
        psA, psB = st.psA, st.psB
        block = ctx.enter_context(nc.Block())

        @block.gpsimd
        def _(pool):
            def gathers(g, slot):
                pool.wait_ge(s["summed"], EG * g + EG)
                if take_rel:
                    pool.wait_ge(s["rel"], g + 1)
                pool.sem_inc(s["fence"], 1)
                nc.gpsimd.tensor_copy(gidx[:, slot, :], st.src_i[:, bass.ds(g * EG, EG)]
                                      ).then_inc(s["idx_copied"], 1)
                pool.wait_ge(s["idx_copied"], g + 1)
                pool.sem_inc(s["fence"], 1)
                for j in range(EG):
                    nc.gpsimd.indirect_dma_start(rows[:, slot, j, :], None, table[:, :],
                                                 bass.IndirectOffsetOnAxis(gidx[:, slot, j:j + 1], 0)
                                                 ).then_inc(rows_in[slot], 16)

            def retire(slot, i):
                pool.wait_ge(scat[slot], 16 * EG * (i + 1))
                pool.sem_inc(s["sums_free"], 1)

            def scatters(g, slot, midway=None):
                nc.gpsimd.tensor_copy(sidx[:, slot, :], st.sidx_i[:, bass.ds(g * EG, EG)]
                                      ).then_inc(s["sidx_copied"], 1)
                pool.wait_ge(s["sidx_copied"], g + 1)
                pool.wait_ge(s["summed"], EG * g + EG + 2 * EG)
                pool.sem_inc(s["fence"], 1)
                for j in range(EG):
                    if j == 3 and midway is not None:
                        retire(*midway)
                    nc.gpsimd.indirect_dma_start(agg[:, :], bass.IndirectOffsetOnAxis(sidx[:, slot, j:j + 1], 0),
                                                 sums[:, slot, j, :], None, bounds_check=st.NR - 1,
                                                 oob_is_err=False).then_inc(scat[slot], 16)

            if weighted:
                scatters(0, 0)
                with pool.Fori(0, NG // 2 - 1) as i:
                    scatters(2 * i + 1, 1, midway=(0, i))
                    scatters(2 * i + 2, 0, midway=(1, i))
                scatters(NG - 1, 1, midway=(0, NG // 2 - 1))
            else:
                gathers(0, 0)
                gathers(1, 1)
                scatters(0, 0)
                with pool.Fori(0, NG // 2 - 1) as i:
                    gathers(2 * i + 2, 0)
                    retire(0, i)
                    scatters(2 * i + 1, 1)
                    gathers(2 * i + 3, 1)
                    retire(1, i)
                    scatters(2 * i + 2, 0)
                retire(0, NG // 2 - 1)
                scatters(NG - 1, 1)
            retire(1, NG // 2 - 1)

        @block.vector
        def _(dve):
            nc.vector.memset(sums[:, 1, EG - 1, :], 0.0).then_inc(s["start"], 1)
            dve.wait_ge(s["start"], 1)
            chain = Steps(s["step"], 6)

            def body(g, slot, i):
                if weighted:
                    dve.wait_ge(v_in[slot], 16 * (i + 1))
                    att = st.alpha[:, :, bass.ds(g * EG, EG)].rearrange("p h t -> p t h")
                    nc.vector.tensor_tensor(rows[:, slot, :, :].rearrange("p t (h c) -> p t h c", h=HEADS),
                                            V[:, slot, :, :].rearrange("p t (h c) -> p t h c", h=HEADS),
                                            att.unsqueeze(3).broadcast_to([P, EG, HEADS, P // HEADS]),
                                            ALU.mult).then_inc(s["weighted"], 1)
                    dve.wait_ge(s["weighted"], g + 3)
                else:
                    dve.wait_ge(rows_in[slot], 16 * EG * (i + 1))
                dve.wait_ge(s["sums_free"], g + 1)
                for j in range(EG):
                    before = sums[:, slot, j - 1, :] if j else sums[:, 1 - slot, EG - 1, :]
                    dve.wait_ge(s["summed"], EG * g + j + 2 * EG)
                    nc.vector.scalar_tensor_tensor(
                        sums[:, slot, j, :], before, st.cont[:, bass.ds(g * EG + j, 1)], rows[:, slot, j, :],
                        ALU.mult, ALU.add).then_inc(s["summed"], 1)
                if take_rel:
                    nc.vector.tensor_tensor(st.rel[:, bass.ds(g * EG, EG)], rows[:, slot, :, P],
                                            st.ew[:, bass.ds(g * EG, EG)], ALU.subtract).then_inc(s["rel"], 1)
                if embed:
                    chain.start(g)
                    a = ang[:, slot, :, :]
                    dve.wait_ge(s["tenc"], g + 1)
                    chain.mark(nc.vector.tensor_tensor(
                        a, st.rel[:, bass.ds(g * EG, EG)].unsqueeze(2).broadcast_to([P, EG, TD]),
                        st.wt[:, :].unsqueeze(1).broadcast_to([P, EG, TD]), ALU.mult))
                    chain.wait(dve)
                    chain.mark(nc.vector.tensor_tensor(
                        a, a, st.bt[:, :].unsqueeze(1).broadcast_to([P, EG, TD]), ALU.add))
                    chain.wait(dve)
                    chain.mark(nc.vector.tensor_scalar(turn[:, :, :], a, 1.0 / (2 * math.pi), MAGIC,
                                                       ALU.mult, ALU.add))
                    chain.wait(dve)
                    chain.mark(nc.vector.tensor_scalar(turn[:, :, :], turn[:, :, :], MAGIC, None, ALU.subtract))
                    chain.wait(dve)
                    chain.mark(nc.vector.scalar_tensor_tensor(a, turn[:, :, :], -TWO_PI_HI, a, ALU.mult, ALU.add))
                    chain.wait(dve)
                    chain.mark(nc.vector.scalar_tensor_tensor(a, turn[:, :, :], -TWO_PI_LO, a, ALU.mult, ALU.add))
                    chain.wait(dve)
                    nc.vector.scalar_tensor_tensor(a, a, -1.0, a, ALU.mult, ALU.max).then_inc(s["ang"], 1)
                    chain.end()

            edge_groups(dve, NG, body)
            dve.wait_ge(s["summed"], EG * NG + 2 * EG)
            nc.vector.tensor_copy(st.tail[:, 0:cols], sums[:, 1, EG - 1, :]).then_inc(s["tail"], 1)

        if take_rel:
            @block.sync
            def _(sp):
                for k in range(ZPARTS):
                    if k > 0:
                        sp.wait_ge(s["summed"], EG * (NG * k // ZPARTS) + 2 * EG)
                    zero_part(st, sp, st.agg, P, k)
                    if k < MPARTS:
                        message_part(st, sp, k)
                sp.wait_ge(st.filled, 16 * (st.NGROUPS + 1 + ZPARTS + MPARTS))

        if weighted:
            @block.sync
            def _(sp):
                def body(g, slot, i):
                    sp.wait_ge(s["weighted"], g + 1)
                    sp.dma_start(V[:, slot, :, :],
                                 st.vj[:, bass.ds(g * EG, EG), :]).then_inc(v_in[slot], 16)
                edge_groups(sp, NG, body)

        if not embed:
            return

        @block.sync
        def _(sp):
            def load(g, slot):
                sp.dma_start(EA[:, slot, :, TD:TD + MD],
                             st.msg.rearrange("(p t) d -> p t d", p=P)[:, bass.ds(g * EG, EG), :]
                             ).then_inc(msg_in[slot], 16)

            def store(g, slot):
                sp.wait_ge(s["e_out"], 4 * g + 4 + 4)
                for c in range(2):
                    sp.dma_start(st.e[c][:, bass.ds(g * EG, EG), :],
                                 EB[:, slot, :, c * P:(c + 1) * P]).then_inc(e_st[slot], 16)

            def load_next_then_store(g, slot):
                sp.wait_ge(s["tposed"], EG * g + EG + 2 * EG)
                load(g + 2, slot)
                store(g, slot)

            def retire(slot, i):
                sp.wait_ge(e_st[slot], 32 * (i + 1))
                sp.sem_inc(s["eb_free"], 1)

            load(0, 0)
            load(1, 1)
            load_next_then_store(0, 0)
            with sp.Fori(0, NG // 2 - 2) as i:
                load_next_then_store(2 * i + 1, 1)
                retire(0, i)
                load_next_then_store(2 * i + 2, 0)
                retire(1, i)
            load_next_then_store(NG - 3, 1)
            retire(0, NG // 2 - 2)
            store(NG - 2, 0)
            retire(1, NG // 2 - 2)
            store(NG - 1, 1)
            retire(0, NG // 2 - 1)
            retire(1, NG // 2 - 1)

        @block.scalar
        def _(act):
            def body(g, slot, i):
                act.wait_ge(s["ang"], g + 3)
                act.wait_ge(s["tposed"], EG * g + EG)
                act.activation(EA[:, slot, :, 0:TD], ang[:, slot, :, :], ACT.Sin, scale=-1.0,
                               bias=st.half_pi[:, 0:1]).then_inc(s["tenc"], 1)
                for half in range(2):
                    n = (4 if half == 0 else EG - 4) * P
                    act.wait_ge(s["tposed"], EG * g + (4 if half == 0 else EG) + 2 * EG)
                    act.wait_ge(s["e_done"], 4 * g + 4)
                    act.activation(eaT[:, slot, half * BANK:half * BANK + n], psA[:, 2 * slot + half, 0:n],
                                   ACT.Copy).then_inc(s["eat"], 1)
                for b in range(4):
                    n = min(2, EG - 2 * b)
                    act.wait_ge(s["e_done"], 4 * g + b + 1 + 8)
                    act.wait_ge(s["eb_free"], g + 1)
                    act.activation(EB[:, slot, 2 * b:2 * b + n, :],
                                   psB[:, b, 0:n * 2 * P].rearrange("p (t d) -> p t d", d=2 * P),
                                   ACT.Copy).then_inc(s["e_out"], 1)
            edge_groups(act, NG, body)

        @block.tensor
        def _(pe):
            def body(g, slot, i):
                pe.wait_ge(s["tenc"], g + 3)
                pe.wait_ge(msg_in[slot], 16 * (i + 1))
                pe.wait_ge(s["eat"], 2 * g + 2)
                for j in range(EG):
                    nc.tensor.transpose(psA[:, 2 * slot + j // 4, (j % 4) * P:(j % 4 + 1) * P],
                                        EA[:, slot, j, :], st.ident[:, :]).then_inc(s["tposed"], 1)
                for b in range(4):
                    if b in (0, 2):
                        pe.wait_ge(s["eat"], 2 * g + b // 2 + 1 + 4)
                    pe.wait_ge(s["e_out"], 4 * g + b + 1)
                    for j in range(2 * b, min(2 * b + 2, EG)):
                        ins = nc.tensor.matmul(psB[:, b, (j % 2) * 2 * P:(j % 2 + 1) * 2 * P],
                                               eaT[:, slot, j * P:(j + 1) * P], st.we[:, :],
                                               start=True, stop=True)
                    ins.then_inc(s["e_done"], 1)
            edge_groups(pe, NG, body)


def carry_phase(nc, st, agg, cols):
    s = fresh_semaphores(nc, st, ["c", "sum"], gpsimd_dma=("got", "put"))
    with ExitStack() as ctx:
        row = ctx.enter_context(nc.sbuf_tensor(f"row_{st.phase}", [P, cols], F32))
        block = ctx.enter_context(nc.Block())

        @block.tensor
        def _(pe):
            nc.tensor.matmul(st.psA[:, 0, 0:cols], st.carry[:, :], st.tail[:, 0:cols],
                             start=True, stop=True).then_inc(s["c"], 1)

        @block.gpsimd
        def _(pool):
            nc.gpsimd.indirect_dma_start(row[:, :], None, agg[:, :],
                                         bass.IndirectOffsetOnAxis(st.carry_from[:, 0:1], 0)
                                         ).then_inc(s["got"], 16)
            pool.wait_ge(s["sum"], 1)
            nc.gpsimd.indirect_dma_start(agg[:, :], bass.IndirectOffsetOnAxis(st.carry_to[:, 0:1], 0),
                                         row[:, :], None, bounds_check=st.NR - 1,
                                         oob_is_err=False).then_inc(s["put"], 16)
            pool.wait_ge(s["put"], 16)

        @block.vector
        def _(dve):
            dve.wait_ge(s["c"], 1)
            dve.wait_ge(s["got"], 16)
            nc.vector.tensor_tensor(row[:, :], row[:, :], st.psA[:, 0, 0:cols], ALU.add).then_inc(s["sum"], 1)


def score_phase(nc, st, conv):
    EC, NG = st.EC, st.EC // EG
    names = ["idx_copied", "fence", "scored", "v_ready", "step", "e0", "e1", "v_st0", "v_st1", "v_free"]
    s = fresh_semaphores(nc, st, names, dict(scored=2, v_ready=2, v_free=2),
                         gpsimd_dma=("got0", "got1"))
    got, e_in, v_st = (s["got0"], s["got1"]), (s["e0"], s["e1"]), (s["v_st0"], s["v_st1"])
    scale = 1.0 / math.sqrt(P // HEADS)
    with ExitStack() as ctx:
        sb = lambda n, sh, d=F32: ctx.enter_context(nc.sbuf_tensor(f"{n}_{st.phase}", sh, d))
        idx = sb("idx", [P, 2, 2, EG], I32)
        KV = sb("KV", [P, 2, EG, 2 * P])
        Q = sb("Q", [P, 2, EG, P])
        Eb = sb("Eb", [P, 2, EG, P])
        V = sb("V", [P, 2, EG, P])
        dots = sb("dots", [P, 2, EG * HEADS])
        block = ctx.enter_context(nc.Block())

        @block.gpsimd
        def _(pool):
            def body(g, slot, i):
                pool.wait_ge(s["scored"], g + 1)
                pool.sem_inc(s["fence"], 1)
                for side, index in ((0, st.src_i), (1, st.qidx_i)):
                    nc.gpsimd.tensor_copy(idx[:, slot, side, :], index[:, bass.ds(g * EG, EG)]
                                          ).then_inc(s["idx_copied"], 1)
                pool.wait_ge(s["idx_copied"], 2 * g + 2)
                pool.sem_inc(s["fence"], 1)
                for j in range(EG):
                    nc.gpsimd.indirect_dma_start(KV[:, slot, j, :], None, st.kv[:, :],
                                                 bass.IndirectOffsetOnAxis(idx[:, slot, 0, j:j + 1], 0)
                                                 ).then_inc(got[slot], 16)
                    nc.gpsimd.indirect_dma_start(Q[:, slot, j, :], None, st.q[:, :],
                                                 bass.IndirectOffsetOnAxis(idx[:, slot, 1, j:j + 1], 0)
                                                 ).then_inc(got[slot], 16)
            edge_groups(pool, NG, body)

        @block.sync
        def _(sp):
            def load(g, slot):
                sp.dma_start(Eb[:, slot, :, :], st.e[conv][:, bass.ds(g * EG, EG), :]).then_inc(e_in[slot], 16)

            def store(g, slot):
                sp.wait_ge(s["v_ready"], g + 3)
                sp.dma_start(st.vj[:, bass.ds(g * EG, EG), :], V[:, slot, :, :]).then_inc(v_st[slot], 16)

            def store_then_load(g, slot):
                store(g, slot)
                sp.wait_ge(s["scored"], g + 3)
                load(g + 2, slot)

            def retire(slot, i):
                sp.wait_ge(v_st[slot], 16 * (i + 1))
                sp.sem_inc(s["v_free"], 1)

            load(0, 0)
            load(1, 1)
            store_then_load(0, 0)
            with sp.Fori(0, NG // 2 - 2) as i:
                store_then_load(2 * i + 1, 1)
                retire(0, i)
                store_then_load(2 * i + 2, 0)
                retire(1, i)
            store_then_load(NG - 3, 1)
            retire(0, NG // 2 - 2)
            store(NG - 2, 0)
            retire(1, NG // 2 - 2)
            store(NG - 1, 1)
            retire(0, NG // 2 - 1)
            retire(1, NG // 2 - 1)

        @block.vector
        def _(dve):
            chain = Steps(s["step"], 3)

            def body(g, slot, i):
                chain.start(g)
                dve.wait_ge(got[slot], 32 * EG * (i + 1))
                dve.wait_ge(e_in[slot], 16 * (i + 1))
                dve.wait_ge(s["v_free"], g + 1)
                nc.vector.tensor_tensor(V[:, slot, :, :], KV[:, slot, :, P:2 * P], Eb[:, slot, :, :],
                                        ALU.add).then_inc(s["v_ready"], 1)
                k = KV[:, slot, :, 0:P]
                chain.mark(nc.vector.tensor_tensor(k, k, Eb[:, slot, :, :], ALU.add))
                chain.wait(dve)
                chain.mark(nc.vector.tensor_tensor(Q[:, slot, :, :], k, Q[:, slot, :, :], ALU.mult))
                chain.wait(dve)
                chain.mark(nc.vector.tensor_reduce(
                    dots[:, slot, :], Q[:, slot, :, :].rearrange("p t (h c) -> p (t h) c", h=HEADS),
                    AX.X, ALU.add))
                chain.wait(dve)
                nc.vector.tensor_scalar(st.alpha[:, :, bass.ds(g * EG, EG)].rearrange("p h t -> p t h"),
                                        dots[:, slot, :].rearrange("p (t h) -> p t h", h=HEADS), scale, None,
                                        ALU.mult).then_inc(s["scored"], 1)
                chain.end()
            edge_groups(dve, NG, body)


def softmax_phase(nc, st):
    EC = st.EC
    s = fresh_semaphores(nc, st, ["step", "d", "m", "e", "x", "t", "u"])
    H = HEADS
    with ExitStack() as ctx:
        sb = lambda n, sh, d=F32: ctx.enter_context(nc.sbuf_tensor(f"{n}_{st.phase}", sh, d))
        fwd = sb("fwd", [P, H, EC])
        seg = sb("seg", [P, H, EC])
        diag = sb("diag", [P, 2 * H, P])
        cand = sb("cand", [P, 2, 2 * H, P])
        top = sb("top", [P, 2, H])
        both = sb("both", [P, 2, 2 * H])
        part = sb("part", [P, 2 * H])
        pen_in = sb("pen_in", [P, 2, EC])
        out_of = sb("out_of", [P, 2, EC])
        first_only, ends_here = sb("first_only", [P, EC]), sb("ends_here", [P, EC])
        block = ctx.enter_context(nc.Block())
        inside = (st.in_first, st.in_last)

        @block.vector
        def _(dve):
            chain = Steps(s["step"], 999)
            chain.start(0)

            def link(ins):
                chain.mark(ins)
                chain.wait(dve)

            for side in range(2):
                link(nc.vector.tensor_scalar(pen_in[:, side, :], inside[side][:, :], BIG, -BIG,
                                             ALU.mult, ALU.add))
                link(nc.vector.tensor_scalar(out_of[:, side, :], inside[side][:, :], -1.0, 1.0,
                                             ALU.mult, ALU.add))
            link(nc.vector.tensor_tensor(first_only[:, :], st.in_first[:, :], out_of[:, 1, :], ALU.mult))
            link(nc.vector.tensor_tensor(out_of[:, 0, :], out_of[:, 0, :], out_of[:, 1, :], ALU.mult))
            link(nc.vector.tensor_scalar(ends_here[:, :], st.contn[:, :], -1.0, 1.0, ALU.mult, ALU.add))
            only_in = (first_only[:, :], st.in_last[:, :])
            for h in range(H):
                link(nc.vector.tensor_tensor_scan(fwd[:, h, :], st.pen[:, :], st.alpha[:, h, :], -BIG,
                                                  ALU.add, ALU.max))
                link(nc.vector.tensor_tensor_scan(seg[:, h, ::-1], st.penn[:, ::-1], fwd[:, h, ::-1], -BIG,
                                                  ALU.add, ALU.max))
                link(nc.vector.tensor_scalar(diag[:, h, :], st.ident[:, :], seg[:, h, 0:1], None, ALU.mult))
                link(nc.vector.tensor_scalar(diag[:, H + h, :], st.ident[:, :], seg[:, h, EC - 1:EC], None,
                                             ALU.mult))
            nc.vector.memset(top[:, :, :], 0.0).then_inc(s["d"], 1)
            dve.wait_ge(s["d"], 1)
            dve.wait_ge(s["m"], 1)
            for side in range(2):
                for other in range(2):
                    link(nc.vector.tensor_tensor(
                        cand[:, side, other * H:(other + 1) * H, :],
                        st.psA[:, other, :].rearrange("p (h q) -> p h q", h=H),
                        st.pen_same[:, 2 * side + other, :].unsqueeze(1).broadcast_to([P, H, P]), ALU.add))
                link(nc.vector.tensor_reduce(both[:, side, :], cand[:, side, :, :], AX.X, ALU.max))
                link(nc.vector.tensor_tensor(top[:, side, :], both[:, side, 0:H], both[:, side, H:2 * H],
                                             ALU.max))
            for h in range(H):
                for side in range(2):
                    link(nc.vector.scalar_tensor_tensor(seg[:, h, :], pen_in[:, side, :], top[:, side, h:h + 1],
                                                        seg[:, h, :], ALU.add, ALU.max))
            link(nc.vector.tensor_tensor(st.alpha[:, :, :], st.alpha[:, :, :], seg[:, :, :], ALU.subtract))
            nc.vector.memset(part[:, :], 0.0).then_inc(s["x"], 1)
            dve.wait_ge(s["x"], 1)
            dve.wait_ge(s["e"], 1)
            for h in range(H):
                link(nc.vector.tensor_tensor_scan(fwd[:, h, :], st.cont[:, :], st.alpha[:, h, :], 0.0,
                                                  ALU.mult, ALU.add))
            link(nc.vector.tensor_tensor(fwd[:, :, :], fwd[:, :, :],
                                         ends_here[:, :].unsqueeze(1).broadcast_to([P, H, EC]), ALU.mult))
            for h in range(H):
                link(nc.vector.tensor_tensor_scan(seg[:, h, ::-1], st.contn[:, ::-1], fwd[:, h, ::-1], 0.0,
                                                  ALU.mult, ALU.add))
            link(nc.vector.tensor_scalar(part[:, 0:H], seg[:, :, 0], 1.0, None, ALU.mult))
            link(nc.vector.tensor_scalar(part[:, H:2 * H], seg[:, :, EC - 1], st.two_ended[:, 0:1], None,
                                         ALU.mult))
            nc.vector.memset(both[:, :, :], 0.0).then_inc(s["t"], 1)
            dve.wait_ge(s["t"], 1)
            dve.wait_ge(s["u"], 1)
            link(nc.vector.tensor_copy(top[:, :, :].rearrange("p s h -> p (s h)"), st.psB[:, 0, 0:2 * H]))
            link(nc.vector.tensor_tensor(seg[:, :, :], seg[:, :, :],
                                         out_of[:, 0, :].unsqueeze(1).broadcast_to([P, H, EC]), ALU.mult))
            for h in range(H):
                for side in range(2):
                    link(nc.vector.scalar_tensor_tensor(seg[:, h, :], only_in[side], top[:, side, h:h + 1],
                                                        seg[:, h, :], ALU.mult, ALU.add))
            link(nc.vector.tensor_scalar(seg[:, :, :], seg[:, :, :], 1e-16, None, ALU.add))
            link(nc.vector.reciprocal(fwd[:, :, :], seg[:, :, :]))
            link(nc.vector.tensor_tensor(st.alpha[:, :, :], st.alpha[:, :, :], fwd[:, :, :], ALU.mult))

        @block.scalar
        def _(act):
            act.wait_ge(s["x"], 1)
            act.activation(st.alpha[:, :, :], st.alpha[:, :, :], ACT.Exp).then_inc(s["e"], 1)

        @block.tensor
        def _(pe):
            pe.wait_ge(s["d"], 1)
            for side in range(2):
                for h in range(H):
                    ins = nc.tensor.matmul(st.psA[:, side, h * P:(h + 1) * P], st.ones[:, :],
                                           diag[:, side * H + h, :], start=True, stop=True)
            ins.then_inc(s["m"], 1)
            pe.wait_ge(s["t"], 1)
            for side in range(2):
                for other in range(2):
                    mask = st.same[:, 2 * other + side, :]
                    ins = nc.tensor.matmul(st.psB[:, 0, side * H:(side + 1) * H], mask,
                                           part[:, other * H:(other + 1) * H],
                                           start=(other == 0), stop=(other == 1))
            ins.then_inc(s["u"], 1)


def build(nc, a, out):
    st = State()
    st.N, D = a["x"].shape
    st.E = a["src"].shape[0]
    st.MD = a["edge_attr_64"].shape[1]
    st.TD = a["L1_gnn_Wt"].shape[1]
    assert D == P and st.TD + st.MD == P
    st.NGROUPS = -(-st.N // (P * NJ))
    st.NR = st.NGROUPS * P * NJ
    st.TAILP = (st.N - (st.NGROUPS - 1) * P * NJ) // NJ
    st.EC = -(-st.E // (P * 2 * EG)) * 2 * EG
    assert st.TAILP * NJ == st.N - (st.NGROUPS - 1) * P * NJ and st.NGROUPS % 2 == 1
    assert st.E // st.EC == P - 1 and st.NR < NO_NODE and st.NR == P * st.EC
    EC, NR, N = st.EC, st.NR, st.N
    dram = lambda n, sh: nc.dram_tensor(n, sh, F32, kind="Internal").ap()
    st.msg = dram("msg_padded", [P * EC, st.MD])
    table0 = dram("table0", [NR, W0COLS])
    table1, table2 = dram("table1", [NR, P]), dram("table2", [NR, P])
    st.agg0, st.agg = dram("agg0", [NR, W0COLS]), dram("agg", [NR, P])
    x1 = dram("x1", [NR, P])
    st.kv, st.q, st.skip = dram("kv", [NR, 2 * P]), dram("q", [NR, P]), dram("skip", [NR, P])
    skip2 = dram("skip2", [NR, P])
    st.e = [dram(f"edge_emb{c}", [P, EC, P]) for c in range(2)]
    st.vj = dram("vj", [P, EC, P])
    with ExitStack() as ctx:
        sb = lambda n, sh, d=F32: ctx.enter_context(nc.sbuf_tensor(n, sh, d))
        st.src_i, st.sidx_i, st.qidx_i = sb("src_i", [P, EC], I32), sb("sidx_i", [P, EC], I32), sb("qidx_i", [P, EC], I32)
        st.dstf, st.ew, st.rel = sb("dstf", [P, EC]), sb("ew", [P, EC]), sb("rel", [P, EC])
        st.cont, st.contn, st.pen, st.penn = (sb(n, [P, EC]) for n in ("cont", "contn", "pen", "penn"))
        st.in_first, st.in_last = sb("in_first", [P, EC]), sb("in_last", [P, EC])
        st.nv, st.inv = sb("nv", [P, NR // P]), sb("inv_deg", [P, NR // P])
        st.alpha = sb("alpha", [P, HEADS, EC])
        st.ident, st.tri, st.ones = sb("ident", [P, P]), sb("tri", [P, P]), sb("ones", [P, P])
        st.carry = sb("carry", [P, P])
        st.same, st.pen_same = sb("same", [P, 4, P]), sb("pen_same", [P, 4, P])
        st.tail = sb("tail", [P, W0COLS])
        st.two_ended = sb("two_ended", [P, 1])
        st.carry_to, st.carry_from = sb("carry_to", [P, 1], I32), sb("carry_from", [P, 1], I32)
        st.eps, st.half_pi = sb("eps", [P, 1]), sb("half_pi", [P, 1])
        st.w = [sb(f"w{i}", [P, P]) for i in range(3)]
        st.w4 = sb("w4", [P, 2, 4 * P])
        st.biases = sb("biases", [P, 11 * P])
        st.b4 = st.biases[:, 0:8 * P].rearrange("p (c n) -> p c n", c=2)
        st.b0 = st.biases[:, 8 * P:11 * P].rearrange("p (c n) -> p c n", c=3)
        st.biases3, st.ones3 = sb("biases3", [3, 11 * P], BF16), sb("ones3", [3, P], BF16)
        st.bias3 = st.biases3[:, 0:8 * P].rearrange("p (c n) -> p c n", c=2)
        st.bias3_sage = st.biases3[:, 8 * P:11 * P].rearrange("p (c n) -> p c n", c=3)
        st.we = sb("we", [P, 2 * P])
        st.gb = sb("gb", [P, 4])
        st.wt, st.bt = sb("wt", [P, st.TD]), sb("bt", [P, st.TD])
        st.psA = ctx.enter_context(nc.psum_tensor("psA", [P, 4, BANK], F32))
        st.psB = ctx.enter_context(nc.psum_tensor("psB", [P, 4, BANK], F32))
        st.pool = [ctx.enter_context(nc.semaphore(f"phase_sem{i}")) for i in range(34)]

        st.phase, st.ctx = 0, ctx
        st.zeros = sb("zeros", [P, EC * W0COLS // ZPARTS])
        st.edge_attr = a["edge_attr_64"]
        st.filled = ctx.enter_context(nc.semaphore("filled"))

        def run(fn, *args, **kw):
            fn(nc, st, *args, **kw)
            nc.all_engine_barrier()
            st.phase += 1

        run(setup_phase, a)
        run(node_phase, "first", resid=a["x"], w=0, bias=0, stores=[(table0, 0, W0COLS)], first_table=True)
        run(segment_sum_phase, table0, W0COLS, st.agg0, take_rel=True)
        run(carry_phase, st.agg0, W0COLS)
        run(node_phase, "deg", agg=st.agg0, add=table0, w=1, bias=1, affine=0, stores=[(table1, 0, P)])
        run(segment_sum_phase, table1, P, st.agg, embed=True)
        run(carry_phase, st.agg, P)
        run(node_phase, "sage", agg=st.agg, add=table1, w=2, bias=2, affine=2, stores=[(table2, 0, P)])
        run(segment_sum_phase, table2, P, st.agg)
        run(carry_phase, st.agg, P)
        tables = lambda skip: [(st.kv, 0, 2 * P), (st.q, 2 * P, 3 * P), (skip, 3 * P, 4 * P)]
        run(node_phase, "sage", agg=st.agg, add=table2, resid=a["x"], wide=0, stores=tables(st.skip),
            final=x1)
        for conv in range(2):
            run(score_phase, conv)
            run(softmax_phase)
            run(segment_sum_phase, None, P, st.agg, weighted=True)
            run(carry_phase, st.agg, P)
            if conv == 0:
                run(node_phase, "conv", agg=st.agg, add=st.skip, wide=1, stores=tables(skip2))
        run(node_phase, "final", agg=st.agg, add=skip2, resid=x1, final=out)


_INS = ["x", "src", "dst", "edge_attr_64", "edge_weight", "node_vec",
        "L0_gnn_W0", "L0_gnn_b0", "L0_gnn_W1", "L0_gnn_b1", "L0_gnn_W2", "L0_gnn_b2",
        "L0_gnn_g0", "L0_gnn_be0", "L0_gnn_g1", "L0_gnn_be1", "L1_gnn_Wt", "L1_gnn_bt",
        "L1_gnn_Wq1", "L1_gnn_bq1", "L1_gnn_Wk1", "L1_gnn_bk1", "L1_gnn_Wv1", "L1_gnn_bv1", "L1_gnn_We1",
        "L1_gnn_Wskip1", "L1_gnn_bskip1", "L1_gnn_Wq2", "L1_gnn_bq2", "L1_gnn_Wk2", "L1_gnn_bk2",
        "L1_gnn_Wv2", "L1_gnn_bv2", "L1_gnn_We2", "L1_gnn_Wskip2", "L1_gnn_bskip2"]


def kernel(**inputs):
    import numpy as _np
    import concourse.bacc as _bacc
    from concourse import mybir as _mybir
    from concourse.bass_utils import run_bass_kernel_spmd as _run

    nc = _bacc.Bacc("TRN2", target_bir_lowering=False, num_devices=1)
    arrays, args = {}, {}
    for name in _INS:
        arr = _np.ascontiguousarray(inputs[name])
        arrays[f"in_{name}"] = arr
        args[name] = nc.dram_tensor(f"in_{name}", arr.shape, _mybir.dt.from_np(arr.dtype), kind="ExternalInput").ap()
    out = nc.dram_tensor("out_0", inputs["x"].shape, F32, kind="ExternalOutput").ap()
    build(nc, args, out)
    r = _run(nc, [arrays], core_ids=[0])
    return r.results[0]["out_0"]
```
